# Optimizing a Trainium2 kernel written in Bass

```python
import numpy as np
import jax
import jax.numpy as jnp

def _softmax(x, axis=-1):
    return jax.nn.softmax(x, axis=axis)

def _gelu(x):
    return jax.nn.gelu(x, approximate=True)

def _silu(x):
    return jax.nn.silu(x)

def _sigmoid(x):
    return jax.nn.sigmoid(x)

def _layernorm(x, axis=-1, eps=1e-05):
    m = jnp.mean(x, axis=axis, keepdims=True)
    v = jnp.var(x, axis=axis, keepdims=True)
    return (x - m) / jnp.sqrt(v + eps)

def _scatter_add(tgt, idx, src, axis=0):
    return tgt.at[idx].add(src)

def _segment_sum(src, seg, n):
    return jax.ops.segment_sum(src, seg, n)
kernel_name = 'mk_adaln_d1_jaxref_r4_82917f'

def setup_inputs(seed: int=0):
    np.random.seed(seed)
    _w = jnp.asarray

    def _L0_attn_setup():
        import jax, jax.numpy as jnp
        import numpy as np
        B, S, DIN, DIM = (1, 1024, 256, 256)
        NH, NKV = (16, 4)
        HD = DIM // NH
        GS = NH // NKV
        key = jax.random.key(seed)
        ks = jax.random.split(key, 5)

        def w(k, shape, fan_in):
            return jax.random.normal(k, shape, jnp.float32) * fan_in ** (-0.5)
        return {'x': jax.random.normal(ks[0], (B, S, DIN), jnp.float32), 'wq': w(ks[1], (DIM, DIN), DIN), 'wk': w(ks[2], (NKV * HD, DIN), DIN), 'wv': w(ks[3], (NKV * HD, DIN), DIN), 'wo': w(ks[4], (DIM, DIM), DIM)}
    _L0_attn_in = _L0_attn_setup()

    def _L0_ffn_setup():
        import jax, jax.numpy as jnp
        import numpy as np
        HIDDEN = 256
        INTER = 1024
        key = jax.random.key(seed)
        k1, k2, k3, k4, k5 = jax.random.split(key, 5)
        hidden_states = jax.random.normal(k1, (4, 512, HIDDEN), dtype=jnp.float32)
        W1 = jax.random.normal(k2, (HIDDEN, INTER), dtype=jnp.float32) * (1.0 / np.sqrt(HIDDEN))
        b1 = jax.random.normal(k3, (INTER,), dtype=jnp.float32) * 0.02
        W2 = jax.random.normal(k4, (INTER, HIDDEN), dtype=jnp.float32) * (1.0 / np.sqrt(INTER))
        b2 = jax.random.normal(k5, (HIDDEN,), dtype=jnp.float32) * 0.02
        return {'hidden_states': hidden_states, 'W1': W1, 'b1': b1, 'W2': W2, 'b2': b2}
    _L0_ffn_in = _L0_ffn_setup()
    _L0_c = _w((lambda *s: np.random.randn(*s).astype(np.float32) * 0.05)(2, 256))
    _L0_wmod = _w((lambda *s: np.random.randn(*s).astype(np.float32) * 0.05)(256, 6 * 256) * 256 ** (-0.5))
    _d = {'L0_attn_x': _L0_attn_in['x'], 'L0_attn_wq': _L0_attn_in['wq'], 'L0_attn_wk': _L0_attn_in['wk'], 'L0_attn_wv': _L0_attn_in['wv'], 'L0_attn_wo': _L0_attn_in['wo'], 'L0_ffn_W1': _L0_ffn_in['W1'], 'L0_ffn_b1': _L0_ffn_in['b1'], 'L0_ffn_W2': _L0_ffn_in['W2'], 'L0_ffn_b2': _L0_ffn_in['b2'], 'L0_c': _L0_c, 'L0_wmod': _L0_wmod}
    _x0 = _d['L0_attn_x']
    _d['L0_attn_x'] = jax.random.normal(jax.random.fold_in(jax.random.key(seed), 1), (2, 2048, 256), dtype=_x0.dtype)
    del _x0
    return _d

def reference(L0_attn_x, L0_attn_wq, L0_attn_wk, L0_attn_wv, L0_attn_wo, L0_ffn_W1, L0_ffn_b1, L0_ffn_W2, L0_ffn_b2, L0_c, L0_wmod):

    def _L0_attn_ref(x, wq, wk, wv, wo):
        import jax, jax.numpy as jnp
        import numpy as np
        B, S, DIN, DIM = (1, 1024, 256, 256)
        NH, NKV = (16, 4)
        HD = DIM // NH
        GS = NH // NKV
        b, s, _ = x.shape
        q = (x @ wq.T).reshape(b, s, NKV, GS, HD)
        k = (x @ wk.T).reshape(b, s, NKV, HD)
        v = (x @ wv.T).reshape(b, s, NKV, HD)
        scale = jnp.asarray(HD ** 0.5, x.dtype)
        att = jnp.einsum('bsgmd,btgd->bgmst', q, k) / scale
        causal = jnp.triu(jnp.ones((s, s), bool), 1)
        att = jnp.where(causal, -jnp.inf, att)
        att = jax.nn.softmax(att, axis=-1)
        ctx = jnp.einsum('bgmst,btgd->bsgmd', att, v).reshape(b, s, DIM)
        return ctx @ wo.T

    def _L0_ffn_ref(hidden_states, W1, b1, W2, b2):
        import jax, jax.numpy as jnp
        import numpy as np
        HIDDEN = 256
        INTER = 1024
        h = jax.nn.relu(jnp.einsum('bsh,hi->bsi', hidden_states, W1) + b1)
        return jnp.einsum('bsi,ih->bsh', h, W2) + b2
    x = L0_attn_x
    mod = (_silu(L0_c) @ L0_wmod).reshape(L0_c.shape[0], 6, 1, -1)
    sa, ca, ga, sb, cb, gb = (mod[:, 0], mod[:, 1], mod[:, 2], mod[:, 3], mod[:, 4], mod[:, 5])
    ga = (2 * (ga >= 0) - 1) * jnp.maximum(jnp.abs(ga), 0.25)
    gb = (2 * (gb >= 0) - 1) * jnp.maximum(jnp.abs(gb), 0.25)
    h = _layernorm(x, axis=-1) * (1 + ca) + sa
    x = x + ga * _L0_attn_ref(h, L0_attn_wq, L0_attn_wk, L0_attn_wv, L0_attn_wo)
    h = _layernorm(x, axis=-1) * (1 + cb) + sb
    x = x + gb * _L0_ffn_ref(h, L0_ffn_W1, L0_ffn_b1, L0_ffn_W2, L0_ffn_b2)
    return x

_drawn_inputs = setup_inputs


def setup_inputs(seed=0):
    import zlib

    import numpy as np

    out = dict(_drawn_inputs(seed))
    spreads = {}
    factors = {'L0_ffn_b1': 8.0, 'L0_ffn_b2': 8.0}
    for name, (base, spread) in spreads.items():
        noise = np.random.default_rng([zlib.crc32(name.encode()), seed]).standard_normal(out[name].shape)
        drawn = base * np.exp(spread * noise) if base else spread * noise
        out[name] = jnp.asarray(drawn.astype(out[name].dtype))
    for name, factor in factors.items():
        out[name] = (out[name] * factor).astype(out[name].dtype)
    return out
```

```python
from contextlib import ExitStack

import numpy as np

import concourse.bass as bass
from concourse import mybir

F32 = mybir.dt.float32
BF16 = mybir.dt.bfloat16
ACT = mybir.ActivationFunctionType
ALU = mybir.AluOpType
AX_X = mybir.AxisListType.X

B, S, D = 2, 2048, 256
HEADS, GROUPS, HD = 16, 4, 16
GH = HEADS // GROUPS
INTER = 1024
EPS = 1e-5
SCALE = float(HD) ** -0.5
P = 128
CHUNK = 512
CT = CHUNK // P
CHUNKS = S // CHUNK
TILES = S // P
DH = D // P
MT = INTER // P
HALF_HEADS = HEADS // DH
Q_PARTS = (0, 0, 0, 1, 1, 2)
K_PARTS = (0, 1, 2, 0, 1, 0)
ROWS = len(Q_PARTS) * HD
SHIFT_ROWS = ROWS + 2
VW = 32
CREDIT = 2
BEGUN = 1
DMA = 16
NEG = -3.0e38
BANKS = 8
MISC = 7
SCORE_BANKS = (0, 1, 2, 3)
MAX_BANKS = (4, 5)
OUT_BANK = 6


def make_plan():
    def maxima(c, g):
        return [("max", c, g, m, i, k) for m in range(GH) for i in range(CT) for k in range(c + 1)]

    def project(c):
        first = [("fill", "xT", c, n) for n in range(DH)]
        return first, [("fill", "q", c, n) for n in range(DH)] + [("fill", "kv", c, 0), ("fill", "v", c, 0)]

    def feed(c):
        wo = [("fill", "ctxT", c, n) for n in range(DH)] + [("fill", "wo", c, n) for n in range(CT // 2)]
        up = [("fill", "hT", c, n) for n in range(DH)] + [("fill", "up", c, n) for n in range(MT)]
        down = [("fill", "down", c, n) for n in range(CT * 2)]
        return wo, up, down

    plan = []
    first, second = project(0)
    plan += [("ln1", 0), ("fill", "mod", 0, 0), ("xn1", 0)] + first + second + [("fill", "mod", 0, 1)]
    plan += maxima(0, 0) + [("maxrows", 0, 0), ("scale",)]
    rounds = [(c, g) for c in range(CHUNKS) for g in range(GROUPS)]
    units = [(c, g, j) for c, g in rounds for j in range(CT * (c + 1))]
    start = {r: units.index((*r, 0)) for r in rounds}
    at = {n: [] for n in range(len(units))}

    for n, (c, g) in enumerate(rounds):
        length = CT * (c + 1)
        pieces = []
        if n:
            pieces.append(("fill", "oT", *rounds[n - 1]))
        if c + 1 < CHUNKS:
            first, second = project(c + 1)
            if g == 0:
                pieces += [("ln1", c + 1)] + pieces[:0]
                pieces.append(("xn1", c + 1))
                pieces += first
            elif g == 1:
                pieces += second
        if c:
            wo, up, down = feed(c - 1)
            if g == 0:
                pieces += wo[:3]
            elif g == 1:
                pieces += wo[3:] + [("ln2", c - 1), ("xn2", c - 1)] + up[:4]
            elif g == 2:
                pieces += up[4:]
            else:
                pieces += down
        for k, piece in enumerate(pieces):
            at[start[(c, g)] + k * length // len(pieces)].append(piece)
    for n in range(1, len(rounds)):
        a, z = max(0, start[rounds[n - 1]] - 2), start[rounds[n]] - 2
        steps = maxima(*rounds[n])
        for k, step in enumerate(steps):
            at[a + k * (z - a) // len(steps)].append(step)
        at[z].append(("maxrows", *rounds[n]))
    for n, unit in enumerate(units):
        plan.append(("unit", *unit))
        plan += at[n]
    wo, up, down = feed(CHUNKS - 1)
    plan += [("last", *units[-1]), ("fill", "oT", *rounds[-1])] + wo
    plan += [("ln2", CHUNKS - 1), ("xn2", CHUNKS - 1)] + up + down
    return plan


def number(plan):
    first = next(n for n, s in enumerate(plan) if s[0] == "unit")
    last = next(n for n, s in enumerate(plan) if s[0] == "last")
    fills, uses = {}, [0] * BANKS
    ring, at = (MISC,) + SCORE_BANKS, 0
    for n, step in enumerate(plan):
        if step[0] != "fill":
            continue
        if step[1] == "down" and step[3] % 4:
            fills[step] = fills[(*step[:3], step[3] - 1)]
            continue
        if first < n < last:
            bank = MISC
        else:
            bank, at = ring[at % len(ring)], at + 1
        fills[step] = (len(set(fills.values())), bank, uses[bank])
        uses[bank] += 1
    return fills, uses


def adaln_block(nc, x, w_q, w_kv, w_o, w_up, b_up, w_down, b_down, cond, w_mod, out):
    plan = make_plan()
    fills, uses = number(plan)
    N_FILLS = len(set(fills.values()))
    N_UNITS = sum(s[0] == "unit" for s in plan)
    N_MAX = sum(s[0] in ("max", "maxrows") for s in plan)
    N_ROUNDS = CHUNKS * GROUPS
    unit_no = {s[1:]: n for n, s in enumerate(s for s in plan if s[0] == "unit")}
    max_no = {s: n for n, s in enumerate(s for s in plan if s[0] in ("max", "maxrows"))}
    diag_no = {u: n for n, u in enumerate(u for u in unit_no if u[2] >= CT * u[0])}
    N_DIAG = len(diag_no)
    assert N_MAX % 2 == 0

    with ExitStack() as ctx:
        def sb(name, shape, dt=F32):
            return ctx.enter_context(nc.sbuf_tensor(name, shape, dt))

        def sem(name):
            return ctx.enter_context(nc.semaphore(name))

        psum = ctx.enter_context(nc.psum_tensor("psum", [P, BANKS, CHUNK], F32))

        wq = sb("wq", [P, DH, D])
        wkv = sb("wkv", [P, DH, P])
        wo = sb("wo", [P, DH, D])
        wup = sb("wup", [P, DH, INTER])
        wdown = sb("wdown", [P, MT, D])
        wmod = sb("wmod", [P, DH, 6 * D])
        bup = sb("bup", [P, MT])
        bdown = sb("bdown", [P, D])
        wo_g = sb("wo_g", [P, DH, D])
        wdown_g = sb("wdown_g", [P, MT, D])
        bdown_g = sb("bdown_g", [P, D])
        cnd = sb("cnd", [P, DH, B])
        cnd_e = sb("cnd_e", [P, DH, B])
        cnd_r = sb("cnd_r", [P, DH, B])
        silu = sb("silu", [P, DH, B])
        silu_rep = sb("silu_rep", [P, DH, P])
        mod = sb("mod", [P, 4 * DH])
        gate = sb("gate", [P, 2 * D])
        gate_pos = sb("gate_pos", [P, 2 * D])
        gate_abs = sb("gate_abs", [P, 2 * D])
        ident = sb("ident", [P, P])
        ident_b = sb("ident_b", [P, P], BF16)
        causal = sb("causal", [P, CHUNK])
        mhalf = sb("mhalf", [P, CT])
        xs = sb("xs", [P, CHUNKS, CT, D])
        stats = sb("stats", [P, CT, 6])
        mv = sb("mv", [P, CT, 2])
        var_eps = sb("var_eps", [P, CT])
        rstd = sb("rstd", [P, CT])
        xn = sb("xn", [P, CT, D])
        hT = sb("hT", [P, DH, CHUNK])
        part = [sb(f"part{n}", [P, DH + 1, CHUNK], BF16) for n in range(3)]
        rest = sb("rest", [P, DH + 1, CHUNK])
        vT = sb("vT", [GROUPS * HD, CHUNK])
        q_stack = sb("q_stack", [P, 2, HEADS, CHUNK], BF16)
        k_stack = sb("k_stack", [P, GROUPS, S], BF16)
        values = sb("values", [P, TILES, GROUPS, VW])
        scratch = sb("scratch", [P, 2, CHUNK])
        row_max = sb("row_max", [P, GH, CT, CHUNKS])
        neg_max = sb("neg_max", [P, GH, CT])
        neg_parts = sb("neg_parts", [P, 2, GH, CT], BF16)
        neg_rows = sb("neg_rows", [2 * GH * CT, P], BF16)
        probs = sb("probs", [P, 2, GH, CHUNK])
        o_sb = sb("o_sb", [P, CHUNK])
        inv_sum = sb("inv_sum", [P, CT, GH])
        ctx_tok = sb("ctx_tok", [P, CT, GROUPS, GH * HD])
        ctxT = sb("ctxT", [P, DH, CHUNK])
        relu = sb("relu", [P, MT, CHUNK])

        s_small = sem("small_loaded")
        s_wmod = sem("wmod_loaded")
        s_wq = sem("wq_loaded")
        s_wffn = sem("wo_wffn_loaded")
        s_x = [sem(f"x_loaded{c}") for c in range(CHUNKS)]
        s_stack = sem("stacks_loaded")
        s_negrow = sem("neg_rows_in_stack")
        s_out = [sem(f"out_stored{c}") for c in range(CHUNKS)]
        s_fill = sem("fill_ready")
        s_drained = [sem(f"bank_drained{n}") for n in range(BANKS)]
        s_max_ready = sem("max_scores_ready")
        s_max_free = sem("max_scores_free")
        s_neg = sem("neg_max_steps")
        s_scores = sem("scores_ready")
        s_exp = sem("exp_done")
        s_masked = sem("masked")
        s_pv = sem("values_done")
        s_o = sem("o_copied")
        s_const = sem("constants_ready")
        s_cleared = sem("constants_cleared")
        s_cexp = sem("cond_exp_ready")
        s_csteps = sem("cond_steps")
        s_silu = sem("silu_ready")
        s_rep = sem("silu_rep_ready")
        s_mod = sem("mod_ready")
        s_gate = sem("gate_steps")
        s_scaled = sem("weights_scaled")
        s_ln = sem("ln_steps")
        s_var = sem("var_ready")
        s_rstd = sem("rstd_ready")
        s_xn = sem("xn_ready")
        s_bias = sem("down_bias_added")
        s_hi = sem("high_part_ready")
        s_mid = sem("mid_part_ready")
        s_lo = sem("low_part_ready")
        s_vT = sem("vT_ready")
        s_apart = sem("waits_standing_alone")
        s_inv = sem("inv_sum_ready")

        STACK_DMAS = len(Q_PARTS) * (DH + 1)

        def bank_of(step):
            return fills[step][1]

        def score_bank(pair):
            return psum[:, 2 * pair:2 * pair + 2, :]

        def unit_columns(c, j):
            return max(0, j - CT * c) * P



        def slices(m, n=P):
            return slice(m * n, (m + 1) * n)

        def fills_before(step):
            return len({fills[s] for s in plan[:plan.index(step)] if s[0] == "fill"})

        def shape_oT(bank):
            return psum[:, bank, :].rearrange("p (i m v) -> p i m v", i=CT, m=GH)

        norms = [s for s in plan if s[0] in ("ln1", "ln2")]
        xns = [s for s in plan if s[0] in ("xn1", "xn2")]
        N_LN = len(norms)
        splits = [(c, n) for c in range(CHUNKS) for n in range(DH + 1)]
        N_SPLIT = len(splits)

        def wait_drained(eng, b, step):
            _, bank, k = fills[step]
            eng.wait_ge(s_drained[bank], b * uses[bank] + k + 1 + BEGUN)

        def wait_filled(eng, b, step):
            eng.wait_ge(s_fill, b * N_FILLS + fills[step][0] + 1 + BEGUN)

        block = ctx.enter_context(nc.Block())

        def wait_apart(eng, semaphore, value):
            eng.wait_ge(semaphore, value)
            eng.sem_inc(s_apart, 1)

        @block.sync
        def _(sp):
            for s in s_out + [s_stack, s_negrow]:
                sp.sem_inc(s, DMA)
            for s in s_drained + [s_fill, s_o, s_scaled]:
                sp.sem_inc(s, BEGUN)
            for k in range(DH):
                sp.dma_start(cnd[:, k, :], cond[k * P:(k + 1) * P, :]).then_inc(s_small, 16)
            sp.dma_start(bup[:], b_up).then_inc(s_small, 16)
            sp.dma_start(bdown[:], b_down.partition_broadcast(P)).then_inc(s_small, 16)

            with sp.Fori(0, B) as b:
                for c in range(CHUNKS):
                    sp.wait_ge(s_out[c], 2 * DMA * b + DMA)
                    sp.dma_start(xs[:, c], x[bass.ds(b, 1), c * CHUNK:(c + 1) * CHUNK, :]
                                 .rearrange("a (t p) d -> p (a t) d", p=P)).then_inc(s_x[c], 16)
                for step in plan:
                    kind = step[0]
                    if kind == "fill" and step[1] in ("q", "kv"):
                        _, what, c, n = step
                        n = n if what == "q" else DH
                        sp.wait_ge(s_lo, b * N_SPLIT + splits.index((c, n)) + 1)
                        for r in range(len(Q_PARTS)):
                            if n < DH:
                                sp.dma_start(q_stack[slices(r, HD), c % 2, slices(n, HALF_HEADS), :],
                                             part[Q_PARTS[r]][:, n, :]).then_inc(s_stack, 16)
                            else:
                                sp.dma_start(k_stack[slices(r, HD), :, slices(c, CHUNK)],
                                             part[K_PARTS[r]][P // 2:P, n, :]).then_inc(s_stack, 16)
                    elif kind == "maxrows":
                        _, c, g = step
                        sp.wait_ge(s_max_free, b * N_MAX + max_no[step] + 1 + CREDIT)
                        sp.dma_start(q_stack[ROWS:SHIFT_ROWS, c % 2, slices(g, GH), :],
                                     neg_rows[:]).then_inc(s_negrow, 16)
                    elif kind == "fill" and step[1] == "down" and step[3] % 4 == 3:
                        _, _, c, n = step
                        wait_drained(sp, b, step)
                        sp.dma_start(out[bass.ds(b, 1), slices(2 * c + n // 4, CHUNK // 2), :]
                                     .rearrange("a (t p) d -> p (a t) d", p=P),
                                     xs[:, c, slices(n // 4, 2), :]).then_inc(s_out[c], 16)
            for c in range(CHUNKS):
                sp.wait_ge(s_out[c], 2 * DMA * B + DMA)

        @block.gpsimd
        def _(pool):
            nc.gpsimd.memset(ident[:], 0.0).then_inc(s_cleared, 1)
            nc.gpsimd.memset(ident_b[:], 0.0).then_inc(s_cleared, 1)
            nc.gpsimd.memset(causal[:], 0.0).then_inc(s_cleared, 1)
            nc.gpsimd.memset(mhalf[:], -0.5).then_inc(s_const, 1)
            pool.wait_ge(s_cleared, 3)
            for m in (ident, ident_b):
                nc.gpsimd.affine_select(out=m[:], in_=m[:], compare_op=ALU.not_equal, fill=1.0, base=0,
                                        pattern=[[-1, P]], channel_multiplier=1).then_inc(s_const, 1)
            nc.gpsimd.affine_select(out=causal[:, CHUNK - P:], in_=causal[:, CHUNK - P:],
                                    compare_op=ALU.is_ge, fill=NEG, base=0,
                                    pattern=[[-1, P]], channel_multiplier=1).then_inc(s_const, 1)

            with pool.Fori(0, B) as b:
                for step in plan:
                    kind = step[0]
                    if kind in ("ln1", "ln2"):
                        n = norms.index(step)
                        pool.wait_ge(s_var, b * N_LN + n + 1)
                        nc.gpsimd.tensor_tensor(rstd[:], var_eps[:], mhalf[:], ALU.pow).then_inc(s_rstd, 1)
                    elif kind == "xn2":
                        c = step[1]
                        pool.wait_ge(s_scaled, 3 * b + 3 + BEGUN)
                        pool.wait_ge(s_xn, b * N_LN + xns.index(step) + 1)
                        nc.gpsimd.tensor_tensor(xs[:, c], xs[:, c],
                                                bdown_g[:].unsqueeze(1).to_broadcast([P, CT, D]),
                                                ALU.add).then_inc(s_bias, 1)
                    elif kind == "scale":
                        pool.wait_ge(s_gate, 5 * (b + 1))
                        pool.wait_ge(s_wffn, 48)
                        pool.wait_ge(s_small, 64)
                        pool.wait_ge(s_fill, b * N_FILLS + BEGUN)
                        nc.gpsimd.tensor_tensor(wo_g[:], wo[:], gate[:, 0:D].unsqueeze(1).to_broadcast([P, DH, D]),
                                                ALU.mult).then_inc(s_scaled, 1)
                        nc.gpsimd.tensor_tensor(bdown_g[:], bdown[:], gate[:, D:2 * D],
                                                ALU.mult).then_inc(s_scaled, 1)
                        nc.gpsimd.tensor_tensor(wdown_g[:], wdown[:],
                                                gate[:, D:2 * D].unsqueeze(1).to_broadcast([P, MT, D]),
                                                ALU.mult).then_inc(s_scaled, 1)
                    elif kind == "fill" and step[1] in ("q", "kv"):
                        _, what, c, n = step
                        n = n if what == "q" else DH
                        k = splits.index((c, n))
                        _, bank, k_bank = fills[step]
                        wait_apart(pool, s_drained[bank], b * uses[bank] + k_bank + 1 + BEGUN)
                        nc.gpsimd.tensor_copy(part[1][:, n, :], rest[:, n, :]).then_inc(s_mid, 1)
                        pool.wait_ge(s_mid, b * N_SPLIT + k + 1)
                        nc.gpsimd.tensor_tensor(part[2][:, n, :], rest[:, n, :], part[1][:, n, :],
                                                ALU.subtract).then_inc(s_lo, 1)
                    elif kind == "unit" and step[1:] in diag_no:
                        u, first = unit_no[step[1:]], unit_columns(step[1], step[3])
                        for pair in range(2):
                            wait_apart(pool, s_exp, b * 2 * N_UNITS + 2 * u + pair + 1 + CREDIT)
                            p = probs[:, u % 2, slices(pair, 2), first:first + P]
                            nc.gpsimd.affine_select(out=p, in_=p, compare_op=ALU.is_ge, fill=0.0, base=0,
                                                    pattern=[[0, 2], [1, P]],
                                                    channel_multiplier=-1).then_inc(s_masked, 1)

        @block.scalar
        def _(act):
            act.dma_start(wmod[:], w_mod.rearrange("(k p) n -> p k n", p=P)).then_inc(s_wmod, 16)
            for w, src, done in ((wq, w_q, s_wq), (wkv, w_kv, s_wq), (wo, w_o, s_wffn),
                                 (wup, w_up, s_wffn), (wdown, w_down, s_wffn)):
                act.dma_start(w[:], src.rearrange("(k p) n -> p k n", p=P)).then_inc(done, 16)
            act.sem_inc(s_exp, CREDIT)
            act.wait_ge(s_small, 64)
            nc.scalar.activation(cnd_e[:], cnd[:], ACT.Exp, scale=-1.0).then_inc(s_cexp, 1)

            with act.Fori(0, B) as b:
                for step in plan:
                    kind = step[0]
                    if kind == "unit":
                        _, c, g, j = step
                        u, first = unit_no[(c, g, j)], unit_columns(c, j)
                        for pair in range(2):
                            act.wait_ge(s_scores, b * 2 * N_UNITS + 2 * u + pair + 1)
                            nc.scalar.activation(probs[:, u % 2, slices(pair, 2), first:],
                                                 score_bank(pair)[:, :, first:], ACT.Exp,
                                                 scale=SCALE).then_inc(s_exp, 1)
                    if kind == "last" or (kind == "unit" and j == 0 and u > 0):
                        n = N_ROUNDS if kind == "last" else GROUPS * c + g
                        act.wait_ge(s_pv, b * N_ROUNDS + n)
                        nc.scalar.activation(o_sb[:], psum[:, OUT_BANK, :], ACT.Copy).then_inc(s_o, 1)
                    if kind != "fill":
                        continue
                    _, what, c, n = step
                    bank = bank_of(step)
                    src, done = psum[:, bank, :], s_drained[bank]
                    if what in ("xT", "hT"):
                        at = 0 if what == "xT" else 2 * DH
                        act.wait_ge(s_mod, 2 * b + 2)
                        wait_filled(act, b, step)
                        nc.scalar.activation(hT[:, n, :], src, ACT.Identity, scale=mod[:, at + DH + n:at + DH + n + 1],
                                             bias=mod[:, at + n:at + n + 1]).then_inc(done, 1)
                    elif what == "q":
                        if n == 0:
                            act.wait_ge(s_stack, (b * CHUNKS + c) * DMA * STACK_DMAS + DMA)
                        wait_filled(act, b, step)
                        nc.scalar.activation(part[0][:, n, :], src, ACT.Copy).then_inc(s_hi, 1)
                    elif what == "kv":
                        wait_filled(act, b, step)
                        nc.scalar.activation(vT[:], psum[0:P // 2, bank, :], ACT.Copy).then_inc(s_vT, 1)
                        nc.scalar.activation(part[0][:, DH, :], src, ACT.Copy).then_inc(s_hi, 1)
                    elif what == "ctxT":
                        wait_filled(act, b, step)
                        nc.scalar.activation(ctxT[:, n, :], src, ACT.Copy).then_inc(done, 1)
                    elif what == "up":
                        wait_filled(act, b, step)
                        nc.scalar.activation(relu[:, n, :], src, ACT.Relu, bias=bup[:, n:n + 1]).then_inc(done, 1)

        @block.vector
        def _(dve):
            dve.sem_inc(s_max_free, CREDIT)
            nc.vector.memset(k_stack[ROWS:SHIFT_ROWS, :, :], 1.0).then_inc(s_const, 1)
            nc.vector.memset(values[:], 1.0).then_inc(s_const, 1)
            dve.wait_ge(s_cexp, 1)
            nc.vector.tensor_scalar(cnd_r[:], cnd_e[:], 1.0, None, ALU.add).then_inc(s_csteps, 1)
            dve.wait_ge(s_csteps, 1)
            nc.vector.reciprocal(cnd_e[:], cnd_r[:]).then_inc(s_csteps, 1)
            dve.wait_ge(s_csteps, 2)
            nc.vector.tensor_tensor(silu[:], cnd[:], cnd_e[:], ALU.mult).then_inc(s_silu, 1)
            dve.wait_ge(s_silu, 1)
            dve.wait_ge(s_const, 6)

            with dve.Fori(0, B) as b:
                dve.wait_ge(s_fill, b * N_FILLS + BEGUN)
                nc.vector.tensor_copy(silu_rep[:], silu[:, :, bass.ds(b, 1)].to_broadcast([P, DH, P])).then_inc(s_rep, 1)
                for step in plan:
                    kind = step[0]
                    if kind == "max":
                        _, c, g, m, i, k = step
                        n = max_no[step]
                        bank = MAX_BANKS[n % 2]
                        to = row_max[:, m, i, k:k + 1]
                        if k < c:
                            dve.wait_ge(s_max_ready, b * N_MAX + n + 1)
                            nc.vector.tensor_reduce(to, psum[:, bank, :], AX_X, ALU.max).then_inc(s_max_free, 1)
                        else:
                            wide = (i + 1) * P
                            wait_apart(dve, s_max_ready, b * N_MAX + n + 1)
                            nc.vector.tensor_tensor_reduce(scratch[:, n % 2, 0:wide], psum[:, bank, 0:wide],
                                                           causal[:, CHUNK - wide:], 1.0, NEG, ALU.add, ALU.max,
                                                           to).then_inc(s_max_free, 1)
                    elif kind == "maxrows":
                        _, c, g = step
                        n, r = max_no[step], GROUPS * c + g
                        dve.wait_ge(s_max_free, b * N_MAX + n + CREDIT)
                        nc.vector.tensor_reduce(neg_max[:], row_max[:, :, :, 0:c + 1], AX_X, ALU.max,
                                                negate=True).then_inc(s_neg, 1)
                        dve.wait_ge(s_neg, b * 3 * N_ROUNDS + 3 * r + 1)
                        nc.vector.tensor_copy(neg_parts[:, 0], neg_max[:]).then_inc(s_neg, 1)
                        dve.wait_ge(s_neg, b * 3 * N_ROUNDS + 3 * r + 2)
                        nc.vector.tensor_tensor(neg_parts[:, 1], neg_max[:], neg_parts[:, 0],
                                                ALU.subtract).then_inc(s_neg, 1)
                        dve.wait_ge(s_negrow, (b * N_ROUNDS + r) * DMA + DMA)
                        dve.wait_ge(s_max_ready, b * N_MAX + n + 1)
                        nc.vector.tensor_copy(neg_rows[:], psum[:].bitcast(BF16)[0:2 * GH * CT, MAX_BANKS[n % 2], 0:P])\
                            .then_inc(s_max_free, 1)
                    elif kind in ("ln1", "ln2"):
                        c, n = step[1], norms.index(step)
                        if kind == "ln1":
                            dve.wait_ge(s_x[c], 16 * b + 16)
                        else:
                            wait_drained(dve, b, ("fill", "wo", c, CT // 2 - 1))
                        for i in range(CT):
                            last = nc.vector.bn_stats(stats[:, i, :], xs[:, c, i, :])
                        last.then_inc(s_ln, 1)
                        wait_apart(dve, s_ln, b * 2 * N_LN + 2 * n + 1)
                        for i in range(CT):
                            last = nc.vector.bn_aggr(mv[:, i, :], stats[:, i, :])
                        last.then_inc(s_ln, 1)
                        dve.wait_ge(s_ln, b * 2 * N_LN + 2 * n + 2)
                        nc.vector.tensor_scalar(var_eps[:], mv[:, :, 1], EPS, None, ALU.add).then_inc(s_var, 1)
                    elif kind in ("xn1", "xn2"):
                        c, n = step[1], xns.index(step)
                        dve.wait_ge(s_rstd, b * N_LN + n + 1)
                        dve.wait_ge(s_fill, b * N_FILLS + fills_before(step) + BEGUN)
                        for i in range(CT):
                            last = nc.vector.tensor_scalar(xn[:, i, :], xs[:, c, i, :], mv[:, i, 0:1],
                                                           rstd[:, i:i + 1], ALU.subtract, ALU.mult)
                        last.then_inc(s_xn, 1)
                    if kind != "fill":
                        continue
                    _, what, c, n = step
                    bank = bank_of(step)
                    done = s_drained[bank]
                    if what == "mod" and n == 0:
                        wait_filled(dve, b, step)
                        to = mod[:].rearrange("p (a s h) -> p a s h", a=2, s=2)
                        of = psum[:, bank, 0:8 * DH].rearrange("p (a s h e) -> p a s h e", a=2, s=2, h=DH)
                        nc.vector.tensor_copy(to[:, :, 0, :], of[:, :, 0, :, 0]).then_inc(s_mod, 1)
                        nc.vector.tensor_scalar(to[:, :, 1, :], of[:, :, 1, :, 0], 1.0, None, ALU.add).then_inc(s_mod, 1)
                        dve.wait_ge(s_mod, 2 * b + 2)
                        dve.sem_inc(done, 1)
                    elif what == "mod":
                        wait_filled(dve, b, step)
                        dve.wait_ge(s_scaled, 3 * b + BEGUN)
                        nc.vector.tensor_scalar(gate_pos[:], psum[:, bank, :], 0.0, 2.0, ALU.is_ge,
                                                ALU.mult).then_inc(s_gate, 1)
                        nc.vector.tensor_copy(gate[:], psum[:, bank, :]).then_inc(s_gate, 1)
                        dve.wait_ge(s_gate, 5 * b + 2)
                        dve.sem_inc(done, 1)
                        nc.vector.scalar_tensor_tensor(gate_abs[:], gate[:], -1.0, gate[:], ALU.mult,
                                                       ALU.max).then_inc(s_gate, 1)
                        dve.wait_ge(s_gate, 5 * b + 3)
                        nc.vector.tensor_scalar(gate_abs[:], gate_abs[:], 0.25, None, ALU.max).then_inc(s_gate, 1)
                        dve.wait_ge(s_gate, 5 * b + 4)
                        nc.vector.scalar_tensor_tensor(gate[:], gate_pos[:], -1.0, gate_abs[:], ALU.add,
                                                       ALU.mult).then_inc(s_gate, 1)
                    elif what in ("q", "kv"):
                        n = n if what == "q" else DH
                        dve.wait_ge(s_hi, b * N_SPLIT + splits.index((c, n)) + 1)
                        nc.vector.tensor_tensor(rest[:, n, :], psum[:, bank, :], part[0][:, n, :],
                                                ALU.subtract).then_inc(done, 1)
                    elif what == "v":
                        wait_filled(dve, b, step)
                        nc.vector.tensor_copy(values[:, slices(c, CT), :, 0:HD],
                                              psum[:, bank, 0:CT * GROUPS * HD]
                                              .rearrange("p (t g d) -> p t g d", t=CT, g=GROUPS)).then_inc(done, 1)
                    elif what == "oT":
                        r = GROUPS * c + n
                        o = shape_oT(bank)
                        wait_filled(dve, b, step)
                        nc.vector.reciprocal(inv_sum[:], o[:, :, :, HD]).then_inc(s_inv, 1)
                        dve.wait_ge(s_inv, b * N_ROUNDS + r + 1)
                        nc.vector.tensor_tensor(ctx_tok[:, :, n, :].rearrange("p i (m d) -> p i m d", m=GH),
                                                o[:, :, :, 0:HD],
                                                inv_sum[:].unsqueeze(3).to_broadcast([P, CT, GH, HD]),
                                                ALU.mult).then_inc(done, 1)
                    elif what == "wo" or (what == "down" and n % 4 == 3):
                        if what == "down":
                            n = n // 4
                            dve.wait_ge(s_bias, b * CHUNKS + c + 1)
                        wait_filled(dve, b, step)
                        to = xs[:, c, slices(n, 2), :]
                        nc.vector.tensor_tensor(to, psum[:, bank, :].rearrange("p (t d) -> p t d", t=2), to,
                                                ALU.add).then_inc(done, 1)

        @block.tensor
        def _(pe):
            pe.wait_ge(s_const, 6)
            pe.wait_ge(s_wmod, 16)
            pe.wait_ge(s_wq, 32)

            def values_of(b, u, c, g, j):
                first = unit_columns(c, j)
                if j == 0:
                    pe.wait_ge(s_o, b * N_ROUNDS + GROUPS * c + g + BEGUN)
                    wait_drained(pe, b, ("fill", "v", c, 0))
                pe.wait_ge(s_exp, b * 2 * N_UNITS + 2 * u + 2 + CREDIT)
                if (c, g, j) in diag_no:
                    pe.wait_ge(s_masked, b * 2 * N_DIAG + 2 * diag_no[(c, g, j)] + 2)
                ends = j == CT * (c + 1) - 1
                for m in range(GH):
                    last = nc.tensor.matmul(psum[slices(m, VW), OUT_BANK, first:], values[:, j, g, :],
                                            probs[:, u % 2, m, first:], start=(j == 0), stop=ends,
                                            skip_group_check=True)
                if ends:
                    last.then_inc(s_pv, 1)

            with pe.Fori(0, B) as b:
                before = None
                for step in plan:
                    kind = step[0]
                    if kind == "unit":
                        _, c, g, j = step
                        u, first = unit_no[(c, g, j)], unit_columns(c, j)
                        if u == 0:
                            for s in plan[:plan.index(step)]:
                                if s[0] == "fill" and bank_of(s) in SCORE_BANKS:
                                    wait_drained(pe, b, s)
                        if j == 0:
                            pe.wait_ge(s_negrow, (b * N_ROUNDS + GROUPS * c + g + 1) * DMA + DMA)
                        for pair in range(2):
                            pe.wait_ge(s_exp, b * 2 * N_UNITS + 2 * u + pair - 1 + CREDIT)
                            for h in range(2 * pair, 2 * pair + 2):
                                last = nc.tensor.matmul(psum[:, SCORE_BANKS[h], first:],
                                                        k_stack[0:SHIFT_ROWS, g, slices(j)],
                                                        q_stack[0:SHIFT_ROWS, c % 2, GH * g + h, first:],
                                                        start=True, stop=True)
                            last.then_inc(s_scores, 1)
                        if before:
                            values_of(b, *before)
                        before = (u, c, g, j)
                    elif kind == "last":
                        values_of(b, *before)
                    elif kind == "max":
                        _, c, g, m, i, k = step
                        n = max_no[step]
                        wide = CHUNK if k < c else (i + 1) * P
                        if (g, m, i, k) == (0, 0, 0, 0):
                            pe.wait_ge(s_stack, (b * CHUNKS + c + 1) * DMA * STACK_DMAS + DMA)
                        pe.wait_ge(s_max_free, b * N_MAX + n - 1 + CREDIT)
                        nc.tensor.matmul(psum[:, MAX_BANKS[n % 2], 0:wide],
                                         q_stack[0:ROWS, c % 2, GH * g + m, slices(i)],
                                         k_stack[0:ROWS, g, k * CHUNK:k * CHUNK + wide],
                                         start=True, stop=True).then_inc(s_max_ready, 1)
                    elif kind == "maxrows":
                        _, c, g = step
                        n = max_no[step]
                        pe.wait_ge(s_neg, b * 3 * N_ROUNDS + 3 * (GROUPS * c + g) + 3)
                        pe.wait_ge(s_max_free, b * N_MAX + n - 1 + CREDIT)
                        nc.tensor.transpose(psum[:].bitcast(BF16)[0:2 * GH * CT, MAX_BANKS[n % 2], 0:P],
                                            neg_parts[:].rearrange("p a m i -> p (a m i)"),
                                            ident_b[:]).then_inc(s_max_ready, 1)
                    if kind != "fill":
                        continue
                    _, what, c, n = step
                    _, bank, k_bank = fills[step]
                    to = psum[:, bank, :]
                    if not (what == "down" and n % 4):
                        pe.wait_ge(s_drained[bank], b * uses[bank] + k_bank + BEGUN)
                    if what == "mod" and n == 0:
                        pe.wait_ge(s_rep, b + 1)
                        for col, (which, half) in enumerate((w, h) for w in (0, 1, 3, 4) for h in range(DH)):
                            for k in range(DH):
                                last = nc.tensor.matmul(to[:, 2 * col:2 * col + 2],
                                                        wmod[:, k, slices(which * DH + half)],
                                                        silu_rep[:, k, 0:2], start=(k == 0), stop=(k == DH - 1))
                    elif what == "mod":
                        for col, which in enumerate((2, 5)):
                            for k in range(DH):
                                last = nc.tensor.matmul(to[:, slices(col, D)], silu_rep[:, k, :],
                                                        wmod[:, k, slices(which, D)],
                                                        start=(k == 0), stop=(k == DH - 1))
                    elif what in ("xT", "hT"):
                        pe.wait_ge(s_xn, b * N_LN + xns.index(("xn1" if what == "xT" else "xn2", c)) + 1)
                        for i in range(CT):
                            last = nc.tensor.transpose(to[:, slices(i)], xn[:, i, slices(n)], ident[:])
                    elif what in ("q", "kv"):
                        for k in range(DH):
                            if n == 0:
                                wait_drained(pe, b, ("fill", "xT", c, k))
                            w = wq[:, k, slices(n)] if what == "q" else wkv[:, k, :]
                            last = nc.tensor.matmul(to, w, hT[:, k, :], start=(k == 0), stop=(k == DH - 1))
                    elif what == "v":
                        wait_apart(pe, s_vT, b * CHUNKS + c + 1)
                        for i in range(CT):
                            last = nc.tensor.transpose(to[:, slices(i, GROUPS * HD)], vT[:, slices(i)],
                                                       ident[0:GROUPS * HD, 0:GROUPS * HD])
                    elif what == "oT":
                        pe.wait_ge(s_o, b * N_ROUNDS + GROUPS * c + n + 1 + BEGUN)
                        for i in range(CT):
                            last = nc.tensor.transpose(to[:, slices(i)], o_sb[:, slices(i)], ident[:])
                    elif what == "ctxT":
                        wait_drained(pe, b, ("fill", "oT", c, GROUPS - 1))
                        for i in range(CT):
                            last = nc.tensor.transpose(to[:, slices(i)],
                                                       ctx_tok[:, i].rearrange("p g d -> p (g d)")[:, slices(n)],
                                                       ident[:])
                    elif what == "wo":
                        pe.wait_ge(s_scaled, 3 * b + 3 + BEGUN)
                        for i in range(2):
                            for k in range(DH):
                                wait_drained(pe, b, ("fill", "ctxT", c, k))
                                last = nc.tensor.matmul(to[:, slices(i, D)], ctxT[:, k, slices(2 * n + i)],
                                                        wo_g[:, k, :], start=(k == 0), stop=(k == DH - 1))
                    elif what == "up":
                        for k in range(DH):
                            if n == 0:
                                wait_drained(pe, b, ("fill", "hT", c, k))
                            last = nc.tensor.matmul(to, wup[:, k, slices(n)], hT[:, k, :],
                                                    start=(k == 0), stop=(k == DH - 1))
                    elif what == "down":
                        i, half = n % 4 // 2, n % 2
                        for k in range(half * MT // 2, (half + 1) * MT // 2):
                            if n < 2:
                                wait_drained(pe, b, ("fill", "up", c, k))
                            last = nc.tensor.matmul(to[:, slices(i, D)], relu[:, k, slices(2 * (n // 4) + i)],
                                                    wdown_g[:, k, :], start=(k == 0), stop=(k == MT - 1))
                    if not (what == "down" and n % 4 < 3):
                        last.then_inc(s_fill, 1)


def kernel(L0_attn_x, L0_attn_wq, L0_attn_wk, L0_attn_wv, L0_attn_wo, L0_ffn_W1, L0_ffn_b1, L0_ffn_W2, L0_ffn_b2,
           L0_c, L0_wmod):
    import concourse.bacc as bacc
    from concourse.bass_utils import run_bass_kernel_spmd

    def by_channel(w, heads):
        return w.reshape(heads, HD, D).transpose(1, 0, 2).reshape(heads * HD, D)

    wq = np.asarray(L0_attn_wq).reshape(DH, HALF_HEADS * HD, D)
    w_q = np.concatenate([by_channel(w, HALF_HEADS) for w in wq], 0).T
    w_kv = np.concatenate([np.asarray(L0_attn_wv), by_channel(np.asarray(L0_attn_wk), GROUPS)], 0).T
    arrays = {
        "x": np.asarray(L0_attn_x), "w_q": w_q, "w_kv": w_kv, "w_o": np.asarray(L0_attn_wo).T,
        "w_up": np.asarray(L0_ffn_W1), "b_up": np.asarray(L0_ffn_b1).reshape(MT, P).T,
        "w_down": np.asarray(L0_ffn_W2), "b_down": np.asarray(L0_ffn_b2),
        "cond": np.asarray(L0_c).T, "w_mod": np.asarray(L0_wmod),
    }
    arrays = {name: np.ascontiguousarray(a) for name, a in arrays.items()}
    nc = bacc.Bacc("TRN2", target_bir_lowering=False, num_devices=1)
    args = [nc.dram_tensor(name, a.shape, mybir.dt.from_np(a.dtype), kind="ExternalInput").ap()
            for name, a in arrays.items()]
    out = nc.dram_tensor("out", (B, S, D), F32, kind="ExternalOutput").ap()
    adaln_block(nc, *args, out)
    r = run_bass_kernel_spmd(nc, [arrays], core_ids=[0])
    return r.results[0]["out"]
```

```python
from contextlib import ExitStack

import numpy as np

import concourse.bass as bass
from concourse import mybir

F32 = mybir.dt.float32
F32R = mybir.dt.float32r
BF16 = mybir.dt.bfloat16
ACT = mybir.ActivationFunctionType
ALU = mybir.AluOpType
AX_X = mybir.AxisListType.X

B, S, D = 2, 2048, 256
HEADS, GROUPS, HD = 16, 4, 16
GH = HEADS // GROUPS
INTER = 1024
EPS = 1e-5
SCALE = float(HD) ** -0.5
P = 128
CHUNK = 512
CT = CHUNK // P
CHUNKS = S // CHUNK
TILES = S // P
DH = D // P
MT = INTER // P
HALF_HEADS = HEADS // DH
Q_PARTS = (0, 0, 0, 1, 1, 2)
K_PARTS = (0, 1, 2, 0, 1, 0)
ROWS = len(Q_PARTS) * HD
SHIFT_ROWS = ROWS + 2
VW = 32
RING = 3
BEGUN = 1
DMA = 16
NEG = -3.0e38
BANKS = 8
MISC = 7
SCORE_BANKS = (0, 1, 2)
MAX_BANKS = (3, 4, 5)
OUT_BANK = 6

SPLIT = ("q", "kv", "up")
PIECES = {"q": DH, "kv": DH, "wo": 2, "up": DH, "down": MT}
GATE_STEPS = 5
PROBS = 3
AHEAD = CHUNKS - 2
SCALES = 6

LEAD = 3.2
LEAD_0 = 4.2
ROWS_LAG = 0.9
VALUES = 1.9
XN = 1
BESIDE = 1.3
FIRST_PROJECT = 7.5
SCALE_BEGIN, SCALE_STEP = 5, 2

WINDOW = 16
HOP = 150
ROW_DMA = 2300
STACK_DMA = 2500


def columns(c, j):
    return CHUNK - max(0, j - CT * c) * P


def te_time(step):
    if step[0] == "scores":
        return columns(step[1], step[3])
    if step[0] == "values":
        return 4 * columns(step[1], step[3])
    if step[0] == "fill":
        return (3 if step[1] in SPLIT else 4) * CHUNK if step[1] in PIECES else 2 * CHUNK
    return 0


def ve_time(step):
    _, c, _, _, i, k = step
    return CHUNK + 64 if k < c else (i + 1) * P + 64


class Model:

    def __init__(self):
        self.pe = self.act = self.dve = self.pool = 0.0
        self.done = {("row", 0, 0): ROW_DMA}
        self.exps, self.frees = [], []
        self.bank = 0.0

    def get(self, *key):
        return self.done.get(key, float("inf"))

    def ready(self, step):
        kind = step[0]
        if kind == "scores":
            _, c, g, j, h = step
            u = self.number[(c, g, j)]
            when = [self.exps[-RING] + HOP] if len(self.exps) >= RING else [0]
            if u >= PROBS:
                when.append(0 if ("values", self.units[u - PROBS]) in self.done else float("inf"))
            if j == h == 0:
                when.append(self.get("row", c, g))
            return max(when)
        if kind == "values":
            _, c, g, j = step
            when = [self.get("probs", c, g, j)]
            if j == 0 and (c, g) != (0, 0):
                when.append(self.get("o", GROUPS * c + g - 1))
            if j == 0 and c:
                when.append(self.get("v", c))
            if j == CT * (c + 1) - 1 and (c, g) != (0, 0):
                when.append(self.get("oT", GROUPS * c + g - 1))
            return max(when)
        if kind == "max":
            _, c, g, m, i, k = step
            when = [self.frees[-RING] + HOP] if len(self.frees) >= RING else [0]
            if (m, i, k) == (0, 0, 0) and c:
                when += [self.get("stack", c, g // (GROUPS // DH)), self.get("stack", c, DH)]
            return max(when)
        if kind == "negmax":
            return self.frees[-1]
        if kind == "maxrows":
            return max(self.get("neg"), self.frees[-RING] + HOP)
        if kind == "ln2":
            return self.get("wo", step[1], step[2] // 2)
        if kind in ("xn1", "xn2"):
            return self.get("rstd", kind[2], step[1])
        if kind == "middle":
            return self.get("rest", step[1], step[2], step[3])
        if kind != "fill":
            return 0
        _, what, c, n, piece = step
        when = [self.bank + HOP if piece == 0 else 0]
        if what in ("xT", "hT"):
            when.append(self.get("xn", "1" if what == "xT" else "2", c))
        elif what == "kv":
            when.append(self.get("h", "xT", c, piece))
        elif what == "v":
            when.append(self.get("vT", c))
        elif what == "oT":
            when.append(self.get("o", GROUPS * c + n))
        elif what == "ctxT":
            when.append(self.get("oT", GROUPS * c + GROUPS - 1))
        elif what == "wo":
            when.append(self.get("ctxT", c, DH - 1))
        elif what == "up" and n == 0:
            when.append(self.get("h", "hT", c, piece))
        elif what == "down" and n == 0 and piece < MT // 2:
            when.append(self.get("relu", c, 2 * piece + 1))
        return max(when)

    def on_act(self, width, ready):
        self.act = max(self.act, ready + HOP) + 52 + 0.83 * width
        return self.act

    def on_dve(self, width, ready):
        self.dve = max(self.dve, ready + HOP) + 65 + 1.04 * width
        return self.dve

    def take(self, step):
        kind, ready = step[0], self.ready(step)
        if kind == "scores":
            _, c, g, j, h = step
            width = columns(c, j)
            self.pe = max(self.pe, ready) + 0.42 * width
            self.exps.append(self.on_act(width, self.pe))
            probs = self.act + HOP
            if j >= CT * c and h % 2:
                self.pool = max(self.pool, self.act + HOP) + 350
                probs = self.pool + HOP
            self.done[("probs", c, g, j)] = probs
            if h < GH - 1:
                del self.done[("probs", c, g, j)]
        elif kind == "values":
            _, c, g, j = step
            self.pe = max(self.pe, ready) + 180 + 1.79 * columns(c, j)
            self.done[("values", step[1:])] = self.pe
            if j == CT * (c + 1) - 1:
                self.done[("o", GROUPS * c + g)] = self.on_act(CHUNK, self.pe) + HOP
        elif kind == "max":
            width = CHUNK if step[5] < step[1] else (step[4] + 1) * P
            self.pe = max(self.pe, ready) + 0.42 * width
            self.frees.append(self.on_dve(width, self.pe))
        elif kind == "negmax":
            self.done[("neg",)] = self.on_dve(250, ready) + HOP
        elif kind == "maxrows":
            self.pe = max(self.pe, ready) + 60
            self.frees.append(self.on_dve(P, self.pe))
            self.done[("row", *step[1:])] = self.dve + ROW_DMA
        elif kind in ("ln1", "ln2"):
            self.on_dve(D, ready)
            if step[2] == CT - 1:
                self.done[("rstd", kind[2], step[1])] = self.on_dve(400, self.dve) + 1500
        elif kind in ("xn1", "xn2"):
            self.done[("xn", kind[2], step[1])] = self.on_act(D, ready) + HOP
            if step[2] < CT - 1:
                del self.done[("xn", kind[2], step[1])]
        elif kind == "middle":
            _, what, c, n = step
            mid = self.on_act(CHUNK, ready)
            self.pool = max(self.pool, mid + HOP) + 1225
            self.done[("stack", c, n if what == "q" else DH)] = self.pool + STACK_DMA
        elif kind == "fill":
            _, what, c, n, piece = step
            if what in SPLIT:
                cost = 650
            else:
                cost = 860 if what in PIECES else 560
            self.pe = max(self.pe, ready) + cost
            if not ends(step):
                return
            if what in ("xT", "hT"):
                self.bank = self.on_act(CHUNK, self.pe)
                self.done[("h", what, c, n)] = self.on_dve(CHUNK, self.on_act(CHUNK, self.act)) + HOP
            elif what in ("q", "kv"):
                if what == "kv":
                    self.done[("vT", c)] = self.on_act(CHUNK, self.pe) + HOP
                self.bank = self.on_dve(CHUNK, self.on_act(CHUNK, self.pe))
                self.done[("rest", what, c, n)] = self.bank
            elif what == "v":
                self.bank = self.done[("v", c)] = self.on_dve(CHUNK // 2, self.pe)
            elif what == "oT":
                self.bank = self.done[("oT", GROUPS * c + n)] = self.on_dve(300, self.on_dve(GH * CT, self.pe))
            elif what in ("ctxT", "up"):
                self.bank = self.done[("ctxT" if what == "ctxT" else "relu", c, n)] = self.on_act(CHUNK, self.pe)
            else:
                self.bank = self.done[(what, c, n)] = self.on_dve(CHUNK, self.pe)


def fit(plan):
    model, fitted = Model(), []
    model.units = [s[1:] for s in plan if s[0] == "values"]
    model.number = {u: n for n, u in enumerate(model.units)}
    stream = {"scores": 0, "values": 1, "max": 2, "negmax": 2, "maxrows": 2}
    queues = [[], [], [], []]
    for place, step in enumerate(plan):
        queues[stream.get(step[0], 3)].append((place, step))
    for q in queues:
        q.reverse()
    while any(queues):
        first = min(q[-1][0] for q in queues if q)
        _, _, q = min((max(model.ready(q[-1][1]), model.pe), q[-1][0], n) for n, q in enumerate(queues)
                      if q and q[-1][0] <= first + WINDOW)
        fitted.append(queues[q].pop()[1])
        model.take(fitted[-1])
    return fitted


def make_plan():
    def fill(what, c, count):
        return [("fill", what, c, n, p) for n in range(count) for p in range(PIECES.get(what, 1))]

    def maxima(c, g):
        return [("max", c, g, m, i, k) for m in range(GH) for i in range(CT) for k in range(c + 1)]

    def project(c):
        steps = fill("kv", c, 1) + fill("q", c, 1) + [("middle", "kv", c, 0)]
        return steps + fill("q", c, DH)[DH:] + [("middle", "q", c, 0)] + fill("v", c, 1) + [("middle", "q", c, 1)]

    def stats(kind, c):
        return [(kind, c, i) for i in range(CT)]

    rounds = [(c, g) for c in range(CHUNKS) for g in range(GROUPS)]
    units = [(c, g, j) for c, g in rounds for j in range(CT * (c + 1))]
    unit_of = {u: n for n, u in enumerate(units)}
    start = {r: unit_of[(*r, 0)] for r in rounds}
    placed = []

    def spread(steps, begin, end):
        for n, step in enumerate(steps):
            placed.append((begin + (n + 0.5) * (end - begin) / len(steps), len(placed), step))

    for u, (c, g, j) in enumerate(units):
        for h in range(GH):
            placed.append((u + h / GH, len(placed), ("scores", c, g, j, h)))
        placed.append((u + VALUES, len(placed), ("values", c, g, j)))
    for n, (c, g) in enumerate(rounds):
        begin, end = start[(c, g)], start[(c, g)] + CT * (c + 1)
        pieces = []
        if n:
            pc, pg = rounds[n - 1]
            pieces += [("fill", "oT", pc, pg, 0)]
        if c + 1 < CHUNKS:
            if g == 0:
                for i in range(CT):
                    placed.append((begin + i / CT, len(placed), ("ln1", c + 1, i)))
                    placed.append((begin + XN + i / CT, len(placed), ("xn1", c + 1, i)))
                pieces += fill("xT", c + 1, DH)
                if c == 0:
                    spread(pieces + project(c + 1), begin + XN + 1, FIRST_PROJECT)
                    pieces = []
            elif g == 1 and c:
                pieces += project(c + 1)
        if c:
            before = c - 1
            if g == 0:
                pieces += fill("ctxT", before, DH) + fill("wo", before, CT // 2)
            elif g == 1:
                for i in range(CT):
                    placed.append((begin + i / CT, len(placed), ("ln2", before, i)))
                    placed.append((begin + XN + i / CT, len(placed), ("xn2", before, i)))
                pieces += fill("hT", before, DH) + fill("up", before, MT)[:MT // 2]
            elif g == 2:
                pieces += fill("up", before, MT)[MT // 2:]
            else:
                pieces += fill("down", before, CT // 2)[:2 * MT if c + 1 < CHUNKS else MT]
        spread(pieces, begin + BESIDE, end)

    due = {r: start[r] - (LEAD if r > (1, 0) else LEAD_0) for r in rounds[1:]}
    for r in rounds[1:]:
        placed.append((due[r], len(placed), ("negmax", *r)))
        placed.append((due[r] + ROWS_LAG, len(placed), ("maxrows", *r)))
    base = sorted(placed)
    middle, begin = [], 0
    for r in rounds[1:]:
        stop = next(n for n, (_, _, s) in enumerate(base) if s == ("negmax", *r))
        window = [s for _, _, s in base[begin:stop]]
        steps = maxima(*r)
        room = sum(te_time(s) for s in window)
        load = sum(ve_time(s) for s in steps)
        spent = asked = 0.0
        for s in window:
            while steps and (asked + ve_time(steps[0]) / 2) / load <= spent / room:
                asked += ve_time(steps[0])
                middle.append(steps.pop(0))
            middle.append(s)
            spent += te_time(s)
        middle += steps
        begin = stop
    middle += [s for _, _, s in base[begin:]]

    for n in range(SCALES):
        unit = SCALE_BEGIN + SCALE_STEP * n
        spot = next(k for k, s in enumerate(middle) if s[0] == "scores" and unit_of[s[1:4]] >= unit)
        middle.insert(spot, ("scale", n))
    middle = [("load", c) for c in range(AHEAD, CHUNKS)] + [("load_back",), ("shifts", 1)] + fit(middle)

    end = CHUNKS - 1
    maxima_0 = maxima(0, 0)
    loads = [("load", c) for c in range(AHEAD)]
    rows = [("negmax", 0, 0), ("maxrows", 0, 0)]
    intro = loads[:1] + [("load_raw", "qkv")] + loads[1:] + [("load_raw", "up")] + stats("ln1", 0)
    intro += [("split", "qkv")] + fill("mod", 0, 1) + [("shifts", 0)] + stats("xn1", 0)
    intro += fill("xT", 0, DH) + project(0) + fill("mod", 0, 2)[1:] + fill("gate", 0, B)
    intro += [("gates",), ("split", "up")] + maxima_0 + rows
    turn = {}
    for ahead_too in (True, False):
        def ahead(steps):
            return steps if ahead_too else []
        up, down = fill("up", end, MT), fill("down", end, CT // 2)
        kept = fill("down", end - 1, CT // 2)[MT:]
        steps = ahead(loads + stats("ln1", 0) + [("shifts", 0)]) + [("fill", "oT", *rounds[-1], 0)]
        steps += ahead(stats("xn1", 0) + kept) + fill("ctxT", end, DH) + ahead(fill("xT", 0, DH))
        steps += fill("wo", end, CT // 2) + stats("ln2", end) + (project(0) if ahead_too else kept)
        steps += stats("xn2", end) + fill("hT", end, DH)
        maxes = ahead(maxima_0)
        for n, piece in enumerate(up):
            steps.append(piece)
            steps += maxes[2 * n:2 * n + 2]
        steps += ahead(rows) + down
        turn[ahead_too] = steps
    return intro, middle + turn[True], middle + turn[False]


def ends(step):
    return step[0] == "fill" and step[4] == PIECES.get(step[1], 1) - 1


class Tally:

    def __init__(self, sections, count, base=0, chosen=None):
        self.base, self.upto, total = base, [], []
        for sec, steps in enumerate(sections):
            upto, sum_ = {}, 0
            for step in steps:
                sum_ += count(step) if count else step in chosen[sec]
                upto[step] = sum_
            self.upto.append(upto)
            total.append(sum_)
        self.intro, self.body = total[0], total[1]

    def value(self, sec, b, k):
        if sec == INTRO:
            return self.base + k
        return b * self.body + (self.intro + self.base + k)

    def before(self, sec, b):
        return self.value(sec, b, 0)

    def at(self, sec, b, step, plus=0):
        return self.value(sec, b, self.upto[sec][step] + plus)


INTRO, BODY, LAST = range(3)


def banks(sections):
    found, ring = [], (MISC,) + SCORE_BANKS
    for steps in sections:
        units = [n for n, s in enumerate(steps) if s[0] == "values"]
        here, turn = {}, 0
        for n, step in enumerate(steps):
            if step[0] == "fill" and step[:4] not in here:
                beside = units and n < units[-1]
                here[step[:4]] = MISC if beside else ring[turn % len(ring)]
                turn += not beside
        found.append(here)
    return found


def adaln_block(nc, x, w_q, w_kv, w_o, w_up, b_up, w_down, b_down, cond, w_mod, out):
    sections = make_plan()
    bank_in = banks(sections)
    units = [s[1:] for s in sections[LAST] if s[0] == "values"]
    unit_no = {u: n for n, u in enumerate(units)}
    diagonal = {u for u in units if u[2] >= CT * u[0]}

    def steps(kind, *rest):
        return lambda s: s[:1 + len(rest)] == (kind, *rest)

    def tally(select, by=1, base=0):
        return Tally(sections, lambda s: by if select(s) else 0, base)

    def last_tile(s, *kinds):
        return s[0] in kinds and s[2] == CT - 1

    def splits(s):
        return ends(s) and s[1] in ("q", "kv")

    def column(s):
        return s[3] if s[1] == "q" else DH

    fills = tally(ends, base=BEGUN)
    drains = []
    for bank in range(BANKS):
        in_bank = [{s for s in here if ends(s) and bank_in[sec][s[:4]] == bank} for sec, here in enumerate(sections)]
        drains.append(Tally(sections, None, BEGUN, in_bank))
    maxes = tally(lambda s: s[0] in ("max", "maxrows"))
    scores = tally(steps("scores"))
    frees = tally(lambda s: s[0] in ("max", "maxrows"), base=RING)
    exps = tally(steps("scores"), base=RING)
    masks = tally(lambda s: s[0] == "scores" and s[1:4] in diagonal and s[4] % 2)
    rounds = tally(lambda s: s[0] == "values" and s[3] == CT * (s[1] + 1) - 1)
    outs = tally(lambda s: s[0] == "values" and s[3] == CT * (s[1] + 1) - 1, base=BEGUN)
    negs = tally(steps("negmax"), 3)
    negrows = tally(steps("maxrows"), DMA, DMA)
    lns = tally(lambda s: last_tile(s, "ln1", "ln2"), 3)
    norms = tally(lambda s: last_tile(s, "ln1", "ln2"))
    rstds = tally(lambda s: last_tile(s, "ln1", "ln2"), 2)
    xns = tally(lambda s: last_tile(s, "xn1", "xn2"))
    projections = tally(splits)
    stacks = [tally(lambda s, n=n: splits(s) and column(s) == n, DMA * len(Q_PARTS), DMA) for n in range(DH + 1)]
    vTs = tally(lambda s: ends(s) and s[1] == "kv")
    oTs = tally(lambda s: ends(s) and s[1] == "oT")
    biases = tally(lambda s: last_tile(s, "xn2"))
    hs = tally(lambda s: ends(s) and s[1] in ("xT", "hT"))
    scaled = tally(steps("scale"))
    shifted = [tally(steps("shifts", n)) for n in range(2)]

    with ExitStack() as ctx:
        def sb(name, shape, dt=F32):
            return ctx.enter_context(nc.sbuf_tensor(name, shape, dt))

        def sem(name):
            return ctx.enter_context(nc.semaphore(name))

        psum = ctx.enter_context(nc.psum_tensor("psum", [P, BANKS, CHUNK], F32))

        wq = [sb(f"wq{n}", [P, DH, D], F32R) for n in range(2)]
        wkv = [sb(f"wkv{n}", [P, DH, P], F32R) for n in range(2)]
        wup = [sb(f"wup{n}", [P, DH, INTER], F32R) for n in range(2)]
        bup = sb("bup", [P, MT])
        wo_g = sb("wo_g", [P, DH, D])
        wdown_g = sb("wdown_g", [P, MT, D])
        bdown_g = sb("bdown_g", [P, D])
        cnd = sb("cnd", [P, DH, B])
        cnd_e = sb("cnd_e", [P, DH, B])
        cnd_r = sb("cnd_r", [P, DH, B])
        silu = sb("silu", [P, DH, B])
        silu_rep = sb("silu_rep", [P, DH, B, P])
        mod = sb("mod", [P, 2, 2 * DH, B])
        shifts = sb("shifts", [P, 2, 2 * DH])
        gate = sb("gate", [P, B, 2 * D])
        ident = sb("ident", [P, P])
        ident_b = sb("ident_b", [P, P], BF16)
        causal = sb("causal", [P, CHUNK])
        mhalf = sb("mhalf", [P, CT])
        mone = sb("mone", [P, DH, B])
        xs = sb("xs", [P, CHUNKS, CT, D])
        stats = sb("stats", [P, CT, 6])
        mv = sb("mv", [P, CT, 2])
        var_eps = sb("var_eps", [P, CT])
        neg_mean = sb("neg_mean", [P, CT])
        rstd = sb("rstd", [P, CT])
        shift = sb("shift", [P, CT])
        xn = sb("xn", [P, CT, D])
        hT = sb("hT", [P, DH, CHUNK])
        h_parts = [sb(f"h_part{n}", [P, DH, CHUNK], F32R) for n in range(2)]
        part = [sb(f"part{n}", [P, DH + 1, CHUNK], BF16) for n in range(3)]
        rest = sb("rest", [P, DH + 1, CHUNK])
        vT = sb("vT", [GROUPS * HD, CHUNK])
        q_stack = sb("q_stack", [P, 2, HEADS, CHUNK], BF16)
        k_stack = sb("k_stack", [P, GROUPS, S], BF16)
        values = sb("values", [P, TILES, GROUPS, VW])
        scratch = sb("scratch", [P, RING, CHUNK], BF16)
        row_max = sb("row_max", [P, GH, CT, CHUNKS])
        neg_max = sb("neg_max", [P, GH, CT])
        neg_parts = sb("neg_parts", [P, 2, GH, CT], BF16)
        neg_rows = sb("neg_rows", [2 * GH * CT, P], BF16)
        probs = sb("probs", [P, PROBS, GH, CHUNK])
        o_sb = sb("o_sb", [P, CHUNK])
        inv_sum = sb("inv_sum", [P, CT, GH])
        ctx_tok = sb("ctx_tok", [P, CT, GROUPS, GH * HD])
        ctxT = sb("ctxT", [P, DH, CHUNK])
        relu = sb("relu", [P, MT, CHUNK])
        wmod = relu[:, 0:6, :].rearrange("p m n -> p (m n)").rearrange("p (k n) -> p k n", k=DH)
        gate_sign, gate_abs = relu[:, 0:B, :], relu[:, B:2 * B, :]
        wup_raw = probs[:, PROBS - 1].rearrange("p h n -> p (h n)").rearrange("p (k n) -> p k n", k=DH)
        wq_raw = probs[:, 0, 0].rearrange("p (k n) -> p k n", k=DH)
        wkv_raw = probs[:, 0, 1, 0:DH * P].rearrange("p (k n) -> p k n", k=DH)

        s_cond = sem("cond_loaded")
        s_wmod = [sem(f"wmod_loaded{n}") for n in range(2)]
        s_raw = {which: sem(f"w_{which}_loaded") for which in ("qkv", "up")}
        s_wback = sem("w_back_loaded")
        s_x = [sem(f"x_loaded{c}") for c in range(CHUNKS)]
        s_stack = [sem(f"stack_loaded{n}") for n in range(DH + 1)]
        s_negrow = sem("neg_rows_in_stack")
        s_out = [sem(f"out_stored{c}") for c in range(CHUNKS)]
        s_fill = sem("fill_ready")
        s_drained = [sem(f"bank_drained{n}") for n in range(BANKS)]
        s_max_ready = sem("max_scores_ready")
        s_max_free = sem("max_scores_free")
        s_neg = sem("neg_max_steps")
        s_scores = sem("scores_ready")
        s_exp = sem("exp_done")
        s_masked = sem("masked")
        s_pv = sem("values_done")
        s_o = sem("o_copied")
        s_const = sem("constants_ready")
        s_cleared = sem("constants_cleared")
        s_cexp = sem("cond_exp_ready")
        s_csteps = sem("cond_steps")
        s_silu = sem("silu_ready")
        s_rep = sem("silu_rep_ready")
        s_mod = sem("mod_ready")
        s_shifts = [sem(f"shifts{n}_ready") for n in range(2)]
        s_gate = sem("gate_steps")
        s_scaled = sem("weights_scaled")
        s_ln = sem("ln_steps")
        s_var = sem("var_ready")
        s_rstd = sem("rstd_ready")
        s_xn = sem("xn_ready")
        s_h_hi = sem("h_high_part_ready")
        s_h = sem("h_low_part_ready")
        s_w_hi = sem("weight_high_part_ready")
        s_w = sem("weight_low_part_ready")
        s_bias = sem("down_bias_added")
        s_hi = sem("high_part_ready")
        s_mid = sem("mid_part_ready")
        s_lo = sem("low_part_ready")
        s_vT = sem("vT_ready")
        s_apart = sem("waits_standing_alone")
        s_inv = sem("inv_sum_ready")

        def unit_columns(c, j):
            return max(0, j - CT * c) * P

        def slices(m, n=P):
            return slice(m * n, (m + 1) * n)

        def fill_end(what, c, n):
            return ("fill", what, c, n, PIECES.get(what, 1) - 1)

        def shape_oT(bank):
            return psum[:, bank, :].rearrange("p (i m v) -> p i m v", i=CT, m=GH)

        def batch_of(sec, b, step):
            ahead = step[0] == "shifts" and step[1] == 0 or step[0] == "ln1" and step[1] == 0 \
                or step[0] == "load" and step[1] < AHEAD
            return b + 1 if sec == BODY and ahead else b

        def ring_wait(eng, semaphore, tally, sec, b, n):
            eng.wait_ge(semaphore, tally.value(sec, b, max(n + 1, RING)))

        def wait_drained(eng, sec, b, what, c, n):
            bank = bank_in[sec][("fill", what, c, n)]
            eng.wait_ge(s_drained[bank], drains[bank].at(sec, b, fill_end(what, c, n)))

        def wait_filled(eng, sec, b, step):
            eng.wait_ge(s_fill, fills.at(sec, b, step))

        def wait_apart(eng, semaphore, value):
            eng.wait_ge(semaphore, value)
            eng.sem_inc(s_apart, 1)

        def split_weights(which):
            return [(wkv, wkv_raw, w_kv), (wq, wq_raw, w_q)] if which == "qkv" else [(wup, wup_raw, w_up)]

        block = ctx.enter_context(nc.Block())

        @block.sync
        def _(sp):
            for s in s_out + s_stack + [s_negrow]:
                sp.sem_inc(s, DMA)
            for s in s_drained + [s_fill, s_o]:
                sp.sem_inc(s, BEGUN)

            def emit(sec, b):
                for step in sections[sec]:
                    kind = step[0]
                    if kind == "load_back":
                        sp.wait_ge(s_fill, fills.before(sec, b))
                        sp.dma_start(wo_g[:], w_o.rearrange("(k p) n -> p k n", p=P)).then_inc(s_wback, DMA)
                        sp.dma_start(bdown_g[:], b_down.partition_broadcast(P)).then_inc(s_wback, DMA)
                        sp.dma_start(wdown_g[:], w_down.rearrange("(k p) n -> p k n", p=P)).then_inc(s_wback, DMA)
                    elif kind == "load":
                        c, of = step[1], batch_of(sec, b, step)
                        sp.wait_ge(s_out[c], 2 * DMA * of + DMA)
                        sp.dma_start(xs[:, c], x[bass.ds(of, 1), slices(c, CHUNK), :]
                                     .rearrange("a (t p) d -> p (a t) d", p=P)).then_inc(s_x[c], DMA)
                    elif kind == "load_raw":
                        for _, raw, src in split_weights(step[1]):
                            sp.dma_start(raw, src.rearrange("(k p) n -> p k n", p=P)).then_inc(s_raw[step[1]], DMA)
                        if step[1] == "up":
                            sp.dma_start(bup[:], b_up).then_inc(s_raw["up"], DMA)
                    elif splits(step) or kind == "middle":
                        what, c = step[1:3]
                        n = column(step)
                        parts = Q_PARTS if n < DH else K_PARTS
                        ready = ((0, s_hi),) if splits(step) else ((1, s_mid), (2, s_lo))
                        for p, written in ready:
                            sp.wait_ge(written, projections.at(sec, b, fill_end(*step[1:4])))
                            for r in (r for r, q in enumerate(parts) if q == p):
                                if n < DH:
                                    sp.dma_start(q_stack[slices(r, HD), c % 2, slices(n, HALF_HEADS), :],
                                                 part[p][:, n, :]).then_inc(s_stack[n], DMA)
                                else:
                                    sp.dma_start(k_stack[slices(r, HD), :, slices(c, CHUNK)],
                                                 part[p][P // 2:P, n, :]).then_inc(s_stack[n], DMA)
                    elif kind == "maxrows":
                        _, c, g = step
                        sp.wait_ge(s_max_free, frees.at(sec, b, step))
                        sp.dma_start(q_stack[ROWS:SHIFT_ROWS, c % 2, slices(g, GH), :],
                                     neg_rows[:]).then_inc(s_negrow, DMA)
                    elif ends(step) and step[1] == "down":
                        _, _, c, n, _ = step
                        wait_drained(sp, sec, b, "down", c, n)
                        sp.dma_start(out[bass.ds(b, 1), slices(2 * c + n, CHUNK // 2), :]
                                     .rearrange("a (t p) d -> p (a t) d", p=P),
                                     xs[:, c, slices(n, 2), :]).then_inc(s_out[c], DMA)

            emit(INTRO, 0)
            with sp.Fori(0, B - 1) as b:
                emit(BODY, b)
            emit(LAST, B - 1)
            for c in range(CHUNKS):
                sp.wait_ge(s_out[c], 2 * DMA * B + DMA)

        @block.gpsimd
        def _(pool):
            nc.gpsimd.memset(ident[:], 0.0).then_inc(s_cleared, 1)
            nc.gpsimd.memset(ident_b[:], 0.0).then_inc(s_cleared, 1)
            nc.gpsimd.memset(causal[:], 0.0).then_inc(s_cleared, 1)
            nc.gpsimd.memset(mhalf[:], -0.5).then_inc(s_const, 1)
            nc.gpsimd.memset(mone[:], -1.0).then_inc(s_const, 1)
            pool.wait_ge(s_cleared, 3)
            for m in (ident, ident_b):
                nc.gpsimd.affine_select(out=m[:], in_=m[:], compare_op=ALU.not_equal, fill=1.0, base=0,
                                        pattern=[[-1, P]], channel_multiplier=1).then_inc(s_const, 1)
            nc.gpsimd.affine_select(out=causal[:, CHUNK - P:], in_=causal[:, CHUNK - P:],
                                    compare_op=ALU.is_ge, fill=NEG, base=0,
                                    pattern=[[-1, P]], channel_multiplier=1).then_inc(s_const, 1)

            nc.gpsimd.memset(values[:], 1.0).then_inc(s_const, 1)
            pool.wait_ge(s_const, 7)
            pool.wait_ge(s_cexp, 1)
            nc.gpsimd.tensor_scalar(cnd_r[:], cnd_e[:], 1.0, None, ALU.add).then_inc(s_csteps, 1)
            pool.wait_ge(s_csteps, 1)
            nc.gpsimd.tensor_tensor(cnd_e[:], cnd_r[:], mone[:], ALU.pow).then_inc(s_csteps, 1)
            pool.wait_ge(s_csteps, 2)
            nc.gpsimd.tensor_tensor(silu[:], cnd[:], cnd_e[:], ALU.mult).then_inc(s_silu, 1)
            pool.wait_ge(s_silu, 1)
            nc.gpsimd.tensor_copy(silu_rep[:], silu[:].unsqueeze(3).to_broadcast([P, DH, B, P])).then_inc(s_rep, 1)

            def emit(sec, b):
                for step in sections[sec]:
                    kind = step[0]
                    if last_tile(step, "ln1", "ln2"):
                        pool.wait_ge(s_var, norms.at(sec, b, step))
                        nc.gpsimd.tensor_tensor(rstd[:], var_eps[:], mhalf[:], ALU.pow).then_inc(s_rstd, 1)
                        pool.wait_ge(s_rstd, rstds.at(sec, b, step, -1))
                        nc.gpsimd.tensor_tensor(shift[:], neg_mean[:], rstd[:], ALU.mult).then_inc(s_rstd, 1)
                    elif last_tile(step, "xn2"):
                        c = step[1]
                        pool.wait_ge(s_xn, xns.at(sec, b, step))
                        if c == 0:
                            pool.wait_ge(s_scaled, scaled.at(sec, b, ("scale", 1)))
                        nc.gpsimd.tensor_tensor(xs[:, c], xs[:, c],
                                                bdown_g[:].unsqueeze(1).to_broadcast([P, CT, D]),
                                                ALU.add).then_inc(s_bias, 1)
                    elif kind == "scale":
                        n = step[1]
                        if n == 0:
                            pool.wait_ge(s_gate, GATE_STEPS)
                            wait_apart(pool, s_wback, 3 * DMA * b + 3 * DMA)
                        ga, gb = (gate[:, bass.ds(b, 1), slices(k, D)] for k in range(2))
                        if n == 0:
                            nc.gpsimd.tensor_tensor(wo_g[:], wo_g[:], ga.to_broadcast([P, DH, D]),
                                                    ALU.mult).then_inc(s_scaled, 1)
                        elif n == 1:
                            nc.gpsimd.tensor_tensor(bdown_g[:].unsqueeze(1), bdown_g[:].unsqueeze(1), gb,
                                                    ALU.mult).then_inc(s_scaled, 1)
                        else:
                            k = slices(n - 2, MT // (SCALES - 2))
                            nc.gpsimd.tensor_tensor(wdown_g[:, k, :], wdown_g[:, k, :],
                                                    gb.to_broadcast([P, MT // (SCALES - 2), D]),
                                                    ALU.mult).then_inc(s_scaled, 1)
                    elif kind == "gates":
                        for n in range(B):
                            wait_drained(pool, sec, b, "gate", 0, n)
                        nc.gpsimd.tensor_scalar(gate_sign, gate[:], 0.0, 2.0, ALU.is_ge, ALU.mult).then_inc(s_gate, 1)
                        pool.wait_ge(s_gate, 1)
                        nc.gpsimd.tensor_scalar(gate_sign, gate_sign, -1.0, None, ALU.add).then_inc(s_gate, 1)
                        pool.wait_ge(s_gate, 2)
                        nc.gpsimd.tensor_tensor(gate_abs, gate_sign, gate[:], ALU.mult).then_inc(s_gate, 1)
                        pool.wait_ge(s_gate, 3)
                        nc.gpsimd.tensor_scalar(gate_abs, gate_abs, 0.25, None, ALU.max).then_inc(s_gate, 1)
                        pool.wait_ge(s_gate, 4)
                        nc.gpsimd.tensor_tensor(gate[:], gate_sign, gate_abs, ALU.mult).then_inc(s_gate, 1)
                    elif step == ("split", "up"):
                        pool.wait_ge(s_w_hi, 3)
                        nc.gpsimd.tensor_tensor(wup[1][:], wup_raw, wup[0][:].bitcast(F32),
                                                ALU.subtract).then_inc(s_w, 1)
                    elif kind == "middle":
                        n = column(step)
                        pool.wait_ge(s_mid, projections.at(sec, b, fill_end(*step[1:])))
                        nc.gpsimd.tensor_tensor(part[2][:, n, :], rest[:, n, :], part[1][:, n, :],
                                                ALU.subtract).then_inc(s_lo, 1)
                    elif kind == "scores" and step[1:4] in diagonal and step[4] % 2:
                        _, c, g, j, h = step
                        u, first = unit_no[(c, g, j)], unit_columns(c, j)
                        wait_apart(pool, s_exp, exps.at(sec, b, step))
                        p = probs[:, u % PROBS, h - 1:h + 1, first:first + P]
                        nc.gpsimd.affine_select(out=p, in_=p, compare_op=ALU.is_ge, fill=0.0, base=0,
                                                pattern=[[0, 2], [1, P]],
                                                channel_multiplier=-1).then_inc(s_masked, 1)

            emit(INTRO, 0)
            with pool.Fori(0, B - 1) as b:
                emit(BODY, b)
            emit(LAST, B - 1)

        @block.scalar
        def _(act):
            act.dma_start(cnd[:], cond.rearrange("(k p) b -> p k b", p=P)).then_inc(s_cond, DMA)
            for n, columns_ in enumerate((slice(0, 2 * D), slice(2 * D, 6 * D))):
                act.dma_start(wmod[:, :, columns_], w_mod.rearrange("(k p) n -> p k n", p=P)[:, :, columns_])\
                    .then_inc(s_wmod[n], DMA)
            act.sem_inc(s_exp, RING)
            act.wait_ge(s_cond, DMA)
            nc.scalar.activation(cnd_e[:], cnd[:], ACT.Exp, scale=-1.0).then_inc(s_cexp, 1)

            def split_high(sec, b, step, n):
                act.wait_ge(s_stack[n], stacks[n].at(sec, b, step, -DMA * len(Q_PARTS)))
                wait_filled(act, sec, b, step)
                bank = bank_in[sec][step[:4]]
                nc.scalar.activation(part[0][:, n, :], psum[:, bank, :], ACT.Copy).then_inc(s_hi, 1)

            def emit(sec, b):
                for step in sections[sec]:
                    kind = step[0]
                    if kind == "scores":
                        _, c, g, j, h = step
                        u, first = unit_no[(c, g, j)], unit_columns(c, j)
                        n = u * GH + h
                        if u == PROBS - 1 and h == 0:
                            act.wait_ge(s_w, 3)
                        act.wait_ge(s_scores, scores.at(sec, b, step))
                        nc.scalar.activation(probs[:, u % PROBS, h, first:], psum[:, SCORE_BANKS[n % RING], first:],
                                             ACT.Exp, scale=SCALE).then_inc(s_exp, 1)
                    elif kind in ("xn1", "xn2"):
                        _, c, i = step
                        if i == 0:
                            act.wait_ge(s_rstd, rstds.at(sec, b, ("ln" + kind[2], c, CT - 1)))
                            act.wait_ge(s_fill, fills.at(sec, b, step))
                        last = nc.scalar.activation(xn[:, i, :], xs[:, c, i, :], ACT.Identity,
                                                    scale=rstd[:, i:i + 1], bias=shift[:, i:i + 1])
                        if i == CT - 1:
                            last.then_inc(s_xn, 1)
                    elif kind == "values" and step[3] == CT * (step[1] + 1) - 1:
                        act.wait_ge(s_pv, rounds.at(sec, b, step))
                        nc.scalar.activation(o_sb[:], psum[:, OUT_BANK, :], ACT.Copy).then_inc(s_o, 1)
                    elif kind == "split":
                        act.wait_ge(s_raw[step[1]], 2 * DMA)
                        for parts, raw, _ in split_weights(step[1]):
                            nc.scalar.activation(parts[0][:], raw, ACT.Copy).then_inc(s_w_hi, 1)
                    elif kind == "middle":
                        wait_drained(act, sec, b, *step[1:])
                        n = column(step)
                        nc.scalar.activation(part[1][:, n, :], rest[:, n, :], ACT.Copy).then_inc(s_mid, 1)
                    if not ends(step):
                        continue
                    _, what, c, n, _ = step
                    bank = bank_in[sec][step[:4]]
                    src, done = psum[:, bank, :], s_drained[bank]
                    if what in ("xT", "hT"):
                        norm = ("xT", "hT").index(what)
                        if c == 0:
                            act.wait_ge(s_shifts[norm], shifted[norm].at(sec, b, ("shifts", norm)))
                        wait_filled(act, sec, b, step)
                        nc.scalar.activation(hT[:, n, :], src, ACT.Identity, scale=shifts[:, norm, DH + n:DH + n + 1],
                                             bias=shifts[:, norm, n:n + 1]).then_inc(done, 1)
                        wait_drained(act, sec, b, what, c, n)
                        nc.scalar.activation(h_parts[0][:, n, :], hT[:, n, :], ACT.Copy).then_inc(s_h_hi, 1)
                    elif what == "q":
                        split_high(sec, b, step, n)
                    elif what == "kv":
                        wait_filled(act, sec, b, step)
                        nc.scalar.activation(vT[:], psum[0:P // 2, bank, :], ACT.Copy).then_inc(s_vT, 1)
                        split_high(sec, b, step, DH)
                    elif what == "ctxT":
                        wait_filled(act, sec, b, step)
                        nc.scalar.activation(ctxT[:, n, :], src, ACT.Copy).then_inc(done, 1)
                    elif what == "gate":
                        wait_filled(act, sec, b, step)
                        nc.scalar.activation(gate[:, n], src, ACT.Copy).then_inc(done, 1)
                    elif what == "up":
                        wait_filled(act, sec, b, step)
                        nc.scalar.activation(relu[:, n, :], src, ACT.Relu, bias=bup[:, n:n + 1]).then_inc(done, 1)

            emit(INTRO, 0)
            with act.Fori(0, B - 1) as b:
                emit(BODY, b)
            emit(LAST, B - 1)

        @block.vector
        def _(dve):
            dve.sem_inc(s_max_free, RING)
            pair_of_ones = float(np.array([0x3F803F80], np.uint32).view(np.float32)[0])
            nc.vector.memset(k_stack[ROWS:SHIFT_ROWS, :, :].bitcast(F32), pair_of_ones).then_inc(s_const, 1)

            def emit(sec, b):
                for step in sections[sec]:
                    kind = step[0]
                    if kind == "max":
                        _, c, g, m, i, k = step
                        n = maxes.upto[sec][step] - 1
                        bank = MAX_BANKS[n % RING]
                        to = row_max[:, m, i, k:k + 1]
                        if k < c:
                            dve.wait_ge(s_max_ready, maxes.at(sec, b, step))
                            nc.vector.tensor_reduce(to, psum[:, bank, :], AX_X, ALU.max).then_inc(s_max_free, 1)
                        else:
                            wide = (i + 1) * P
                            wait_apart(dve, s_max_ready, maxes.at(sec, b, step))
                            nc.vector.tensor_tensor_reduce(scratch[:, n % RING, 0:wide], psum[:, bank, 0:wide],
                                                           causal[:, CHUNK - wide:], 1.0, NEG, ALU.add, ALU.max,
                                                           to).then_inc(s_max_free, 1)
                    elif kind == "negmax":
                        _, c, g = step
                        dve.wait_ge(s_max_free, frees.at(sec, b, ("max", c, g, GH - 1, CT - 1, c)))
                        nc.vector.tensor_reduce(neg_max[:], row_max[:, :, :, 0:c + 1], AX_X, ALU.max,
                                                negate=True).then_inc(s_neg, 1)
                        dve.wait_ge(s_neg, negs.at(sec, b, step, -2))
                        nc.vector.tensor_copy(neg_parts[:, 0], neg_max[:]).then_inc(s_neg, 1)
                        dve.wait_ge(s_neg, negs.at(sec, b, step, -1))
                        nc.vector.tensor_tensor(neg_parts[:, 1], neg_max[:], neg_parts[:, 0],
                                                ALU.subtract).then_inc(s_neg, 1)
                    elif kind == "maxrows":
                        _, c, g = step
                        n = maxes.upto[sec][step] - 1
                        dve.wait_ge(s_negrow, negrows.at(sec, b, step, -DMA))
                        dve.wait_ge(s_max_ready, maxes.at(sec, b, step))
                        transposed = psum[:].bitcast(BF16)[0:2 * GH * CT, MAX_BANKS[n % RING], 0:P]
                        nc.vector.tensor_copy(neg_rows[:], transposed).then_inc(s_max_free, 1)
                    elif kind in ("ln1", "ln2"):
                        _, c, i = step
                        if kind == "ln1":
                            dve.wait_ge(s_x[c], DMA * batch_of(sec, b, step) + DMA)
                        else:
                            wait_drained(dve, sec, b, "wo", c, i // 2)
                        last = nc.vector.bn_stats(stats[:, i, :], xs[:, c, i, :])
                        if i == CT - 1:
                            last.then_inc(s_ln, 1)
                            wait_apart(dve, s_ln, lns.at(sec, b, step, -2))
                            for t in range(CT):
                                last = nc.vector.bn_aggr(mv[:, t, :], stats[:, t, :])
                            last.then_inc(s_ln, 1)
                            dve.wait_ge(s_ln, lns.at(sec, b, step, -1))
                            nc.vector.tensor_scalar(neg_mean[:], mv[:, :, 0], -1.0, None, ALU.mult).then_inc(s_ln, 1)
                            nc.vector.tensor_scalar(var_eps[:], mv[:, :, 1], EPS, None, ALU.add).then_inc(s_var, 1)
                    elif step == ("split", "qkv"):
                        for n, (parts, raw, _) in enumerate(split_weights("qkv")):
                            dve.wait_ge(s_w_hi, n + 1)
                            nc.vector.tensor_tensor(parts[1][:], raw, parts[0][:].bitcast(F32),
                                                    ALU.subtract).then_inc(s_w, 1)
                    elif kind == "shifts":
                        norm = step[1]
                        if sec == INTRO:
                            dve.wait_ge(s_mod, 2)
                        elif norm == 0:
                            wait_drained(dve, sec, b, "xT", CHUNKS - 1, DH - 1)
                        else:
                            bank = bank_in[BODY][("fill", "hT", CHUNKS - 1, DH - 1)]
                            dve.wait_ge(s_drained[bank], drains[bank].before(sec, b))
                        dve.sem_inc(s_apart, 1)
                        nc.vector.tensor_copy(shifts[:, norm, :].unsqueeze(2),
                                              mod[:, norm, :, bass.ds(batch_of(sec, b, step), 1)])\
                            .then_inc(s_shifts[norm], 1)
                    if not ends(step):
                        continue
                    _, what, c, n, _ = step
                    bank = bank_in[sec][step[:4]]
                    done = s_drained[bank]
                    if what == "mod":
                        wait_filled(dve, sec, b, step)
                        of = psum[:, bank, 0:2 * DH * B].rearrange("p (s h e) -> p s h e", s=2, h=DH)
                        nc.vector.tensor_copy(mod[:, n, 0:DH], of[:, 0]).then_inc(s_mod, 1)
                        nc.vector.tensor_scalar(mod[:, n, DH:], of[:, 1], 1.0, None, ALU.add).then_inc(s_mod, 1)
                        dve.wait_ge(s_mod, 2 * n + 2)
                        dve.sem_inc(done, 1)
                    elif splits(step):
                        n = column(step)
                        dve.wait_ge(s_hi, projections.at(sec, b, step))
                        nc.vector.tensor_tensor(rest[:, n, :], psum[:, bank, :], part[0][:, n, :],
                                                ALU.subtract).then_inc(done, 1)
                    elif what == "v":
                        wait_filled(dve, sec, b, step)
                        nc.vector.tensor_copy(values[:, slices(c, CT), :, 0:HD],
                                              psum[:, bank, 0:CT * GROUPS * HD]
                                              .rearrange("p (t g d) -> p t g d", t=CT, g=GROUPS)).then_inc(done, 1)
                    elif what == "oT":
                        o = shape_oT(bank)
                        wait_filled(dve, sec, b, step)
                        nc.vector.reciprocal(inv_sum[:], o[:, :, :, HD]).then_inc(s_inv, 1)
                        dve.wait_ge(s_inv, oTs.at(sec, b, step))
                        nc.vector.tensor_tensor(ctx_tok[:, :, n, :].rearrange("p i (m d) -> p i m d", m=GH),
                                                o[:, :, :, 0:HD],
                                                inv_sum[:].unsqueeze(3).to_broadcast([P, CT, GH, HD]),
                                                ALU.mult).then_inc(done, 1)
                    elif what in ("xT", "hT"):
                        dve.wait_ge(s_h_hi, hs.at(sec, b, step))
                        nc.vector.tensor_tensor(h_parts[1][:, n, :], hT[:, n, :], h_parts[0][:, n, :].bitcast(F32),
                                                ALU.subtract).then_inc(s_h, 1)
                    elif what in ("wo", "down"):
                        if what == "down":
                            dve.wait_ge(s_bias, biases.at(sec, b, ("xn2", c, CT - 1)))
                        wait_filled(dve, sec, b, step)
                        to = xs[:, c, slices(n, 2), :]
                        nc.vector.tensor_tensor(to, psum[:, bank, :].rearrange("p (t d) -> p t d", t=2), to,
                                                ALU.add).then_inc(done, 1)

            emit(INTRO, 0)
            with dve.Fori(0, B - 1) as b:
                emit(BODY, b)
            emit(LAST, B - 1)

        @block.tensor
        def _(pe):
            pe.wait_ge(s_const, 7)

            def split_product(to, w, h, start, stop):
                nc.tensor.matmul(to, w[0], h[0], start=start, stop=False)
                nc.tensor.matmul(to, w[1], h[0], start=False, stop=False)
                return nc.tensor.matmul(to, w[0], h[1], start=False, stop=stop)

            def emit(sec, b):
                for step in sections[sec]:
                    kind = step[0]
                    if kind == "scores":
                        _, c, g, j, h = step
                        first = unit_columns(c, j)
                        n = scores.upto[sec][step] - 1
                        if n == 0:
                            for bank in SCORE_BANKS:
                                pe.wait_ge(s_drained[bank], drains[bank].before(sec, b))
                        if j == 0 and h == 0:
                            pe.wait_ge(s_negrow, negrows.before(sec, b) if c == g == 0
                                       else negrows.at(sec, b, ("maxrows", c, g)))
                        ring_wait(pe, s_exp, scores, sec, b, n)
                        nc.tensor.matmul(psum[:, SCORE_BANKS[n % RING], first:], k_stack[0:SHIFT_ROWS, g, slices(j)],
                                         q_stack[0:SHIFT_ROWS, c % 2, GH * g + h, first:],
                                         start=True, stop=True).then_inc(s_scores, 1)
                    elif kind == "values":
                        _, c, g, j = step
                        u, first = unit_no[(c, g, j)], unit_columns(c, j)
                        if j == 0:
                            pe.wait_ge(s_o, outs.value(sec, b, GROUPS * c + g))
                        if j == 0 and c > 0:
                            wait_drained(pe, sec, b, "v", c, 0)
                        elif u == 0:
                            pe.wait_ge(s_drained[MISC], drains[MISC].before(sec, b))
                        pe.wait_ge(s_exp, exps.at(sec, b, ("scores", c, g, j, GH - 1)))
                        if (c, g, j) in diagonal:
                            pe.wait_ge(s_masked, masks.at(sec, b, ("scores", c, g, j, GH - 1)))
                        done = j == CT * (c + 1) - 1
                        for m in range(GH):
                            last = nc.tensor.matmul(psum[slices(m, VW), OUT_BANK, first:], values[:, j, g, :],
                                                    probs[:, u % PROBS, m, first:], start=(j == 0), stop=done,
                                                    skip_group_check=True)
                        if done:
                            last.then_inc(s_pv, 1)
                    elif kind == "max":
                        _, c, g, m, i, k = step
                        n = maxes.upto[sec][step] - 1
                        wide = CHUNK if k < c else (i + 1) * P
                        if (m, i, k) == (0, 0, 0) and g in (0, GROUPS // DH):
                            half = g // (GROUPS // DH)
                            for what, n_, col in (("q", half, half), ("kv", 0, DH)):
                                pe.wait_ge(s_stack[col], stacks[col].before(sec, b) if c == 0 and g
                                           else stacks[col].at(sec, b, fill_end(what, c, n_)))
                        ring_wait(pe, s_max_free, maxes, sec, b, n)
                        nc.tensor.matmul(psum[:, MAX_BANKS[n % RING], 0:wide],
                                         q_stack[0:ROWS, c % 2, GH * g + m, slices(i)],
                                         k_stack[0:ROWS, g, k * CHUNK:k * CHUNK + wide],
                                         start=True, stop=True).then_inc(s_max_ready, 1)
                    elif kind == "maxrows":
                        _, c, g = step
                        n = maxes.upto[sec][step] - 1
                        pe.wait_ge(s_neg, negs.at(sec, b, ("negmax", c, g)))
                        ring_wait(pe, s_max_free, maxes, sec, b, n)
                        nc.tensor.transpose(psum[:].bitcast(BF16)[0:2 * GH * CT, MAX_BANKS[n % RING], 0:P],
                                            neg_parts[:].rearrange("p a m i -> p (a m i)"),
                                            ident_b[:]).then_inc(s_max_ready, 1)
                    if kind != "fill":
                        continue
                    _, what, c, n, piece = step
                    bank = bank_in[sec][step[:4]]
                    to = psum[:, bank, :]
                    if piece == 0:
                        pe.wait_ge(s_drained[bank], drains[bank].at(sec, b, fill_end(what, c, n), -1))
                    if what == "mod":
                        pe.wait_ge(s_silu, 1)
                        pe.wait_ge(s_wmod[n], DMA)
                        for col, (which, half) in enumerate((3 * n + w, h) for w in range(2) for h in range(DH)):
                            for k in range(DH):
                                last = nc.tensor.matmul(to[:, slices(col, B)], wmod[:, k, slices(which * DH + half)],
                                                        silu[:, k, :], start=(k == 0), stop=(k == DH - 1))
                    elif what == "gate":
                        pe.wait_ge(s_rep, 1)
                        for col, which in enumerate((2, 5)):
                            for k in range(DH):
                                last = nc.tensor.matmul(to[:, slices(col, D)], silu_rep[:, k, n, :],
                                                        wmod[:, k, slices(which, D)],
                                                        start=(k == 0), stop=(k == DH - 1))
                    elif what in ("xT", "hT"):
                        pe.wait_ge(s_xn, xns.at(sec, b, ("xn1" if what == "xT" else "xn2", c, CT - 1)))
                        for i in range(CT):
                            last = nc.tensor.transpose(to[:, slices(i)], xn[:, i, slices(n)], ident[:])
                    elif what in ("q", "kv"):
                        if what == "kv":
                            pe.wait_ge(s_h, hs.at(sec, b, fill_end("xT", c, piece)))
                        if what == "kv" and sec == INTRO:
                            pe.wait_ge(s_w, 2)
                        w = [w[:, piece, slices(n)] for w in (wq if what == "q" else wkv)]
                        last = split_product(to, w, [h[:, piece, :] for h in h_parts], piece == 0, piece == DH - 1)
                    elif what == "v":
                        wait_apart(pe, s_vT, vTs.at(sec, b, fill_end("kv", c, 0)))
                        for i in range(CT):
                            last = nc.tensor.transpose(to[:, slices(i, GROUPS * HD)], vT[:, slices(i)],
                                                       ident[0:GROUPS * HD, 0:GROUPS * HD])
                    elif what == "oT":
                        pe.wait_ge(s_o, outs.value(sec, b, GROUPS * c + n + 1))
                        for i in range(CT):
                            last = nc.tensor.transpose(to[:, slices(i)], o_sb[:, slices(i)], ident[:])
                    elif what == "ctxT":
                        wait_drained(pe, sec, b, "oT", c, GROUPS - 1)
                        for i in range(CT):
                            last = nc.tensor.transpose(to[:, slices(i)],
                                                       ctx_tok[:, i].rearrange("p g d -> p (g d)")[:, slices(n)],
                                                       ident[:])
                    elif what == "wo":
                        if c == 0 and n == 0 and piece == 0:
                            pe.wait_ge(s_scaled, scaled.at(sec, b, ("scale", 0)))
                        for k in range(DH):
                            if n == 0 and piece == 0:
                                wait_drained(pe, sec, b, "ctxT", c, k)
                            last = nc.tensor.matmul(to[:, slices(piece, D)], ctxT[:, k, slices(2 * n + piece)],
                                                    wo_g[:, k, :], start=(k == 0), stop=(k == DH - 1))
                    elif what == "up":
                        if n == 0:
                            pe.wait_ge(s_h, hs.at(sec, b, fill_end("hT", c, piece)))
                            pe.wait_ge(s_w, 3)
                        last = split_product(to, [w[:, piece, slices(n)] for w in wup],
                                             [h[:, piece, :] for h in h_parts], piece == 0, piece == DH - 1)
                    elif what == "down":
                        if c == 0 and n == 0 and piece == 0:
                            pe.wait_ge(s_scaled, scaled.at(sec, b, ("scale", SCALES - 1)))
                        i, quarter = divmod(piece, MT // 2)
                        for k in range(2 * quarter, 2 * quarter + 2):
                            if n == i == 0:
                                wait_drained(pe, sec, b, "up", c, k)
                            last = nc.tensor.matmul(to[:, slices(i, D)], relu[:, k, slices(2 * n + i)],
                                                    wdown_g[:, k, :], start=(k == 0), stop=(k == MT - 1))
                    if ends(step):
                        last.then_inc(s_fill, 1)

            emit(INTRO, 0)
            with pe.Fori(0, B - 1) as b:
                emit(BODY, b)
            emit(LAST, B - 1)


def kernel(L0_attn_x, L0_attn_wq, L0_attn_wk, L0_attn_wv, L0_attn_wo, L0_ffn_W1, L0_ffn_b1, L0_ffn_W2, L0_ffn_b2,
           L0_c, L0_wmod):
    import concourse.bacc as bacc
    from concourse.bass_utils import run_bass_kernel_spmd

    def by_channel(w, heads):
        return w.reshape(heads, HD, D).transpose(1, 0, 2).reshape(heads * HD, D)

    wq = np.asarray(L0_attn_wq).reshape(DH, HALF_HEADS * HD, D)
    w_q = np.concatenate([by_channel(w, HALF_HEADS) for w in wq], 0).T
    w_kv = np.concatenate([np.asarray(L0_attn_wv), by_channel(np.asarray(L0_attn_wk), GROUPS)], 0).T
    arrays = {
        "x": np.asarray(L0_attn_x), "w_q": w_q, "w_kv": w_kv, "w_o": np.asarray(L0_attn_wo).T,
        "w_up": np.asarray(L0_ffn_W1), "b_up": np.asarray(L0_ffn_b1).reshape(MT, P).T,
        "w_down": np.asarray(L0_ffn_W2), "b_down": np.asarray(L0_ffn_b2),
        "cond": np.asarray(L0_c).T, "w_mod": np.asarray(L0_wmod),
    }
    arrays = {name: np.ascontiguousarray(a) for name, a in arrays.items()}
    nc = bacc.Bacc("TRN2", target_bir_lowering=False, num_devices=1)
    args = [nc.dram_tensor(name, a.shape, mybir.dt.from_np(a.dtype), kind="ExternalInput").ap()
            for name, a in arrays.items()]
    out = nc.dram_tensor("out", (B, S, D), F32, kind="ExternalOutput").ap()
    adaln_block(nc, *args, out)
    r = run_bass_kernel_spmd(nc, [arrays], core_ids=[0])
    return r.results[0]["out"]
```
